# Optimizing a Trainium2 kernel written in Bass

```python
import numpy as np
import jax
import jax.numpy as jnp

def _softmax(x, axis=-1):
    return jax.nn.softmax(x, axis=axis)

def _gelu(x):
    return jax.nn.gelu(x, approximate=True)

def _silu(x):
    return jax.nn.silu(x)

def _sigmoid(x):
    return jax.nn.sigmoid(x)

def _layernorm(x, axis=-1, eps=1e-05):
    m = jnp.mean(x, axis=axis, keepdims=True)
    v = jnp.var(x, axis=axis, keepdims=True)
    return (x - m) / jnp.sqrt(v + eps)

def _scatter_add(tgt, idx, src, axis=0):
    return tgt.at[idx].add(src)

def _segment_sum(src, seg, n):
    return jax.ops.segment_sum(src, seg, n)
kernel_name = 'mk_seq_preln_d2_jaxref_r8_575312'

def setup_inputs(seed: int=0):
    np.random.seed(seed)
    _w = jnp.asarray

    def _L0_attn_setup():
        import jax, jax.numpy as jnp
        import numpy as np
        HIDDEN = 256
        N_HEADS = 16
        N_KV_HEADS = 4
        HEAD_DIM = HIDDEN // N_HEADS
        ROPE_THETA = 10000.0
        B, S = (1, 256)

        def _apply_rope(x, position_ids, theta=ROPE_THETA):
            b, s, h, hd = x.shape
            dim_half = hd // 2
            inv_freq = 1.0 / theta ** (jnp.arange(0, dim_half, 2, dtype=jnp.float32) / dim_half)
            freqs = position_ids[:, :, None].astype(jnp.float32) * inv_freq[None, None, :]
            cos = jnp.cos(freqs)[:, :, None, :]
            sin = jnp.sin(freqs)[:, :, None, :]
            x_rot = x[..., :dim_half].reshape(b, s, h, dim_half // 2, 2)
            x0, x1 = (x_rot[..., 0], x_rot[..., 1])
            rotated = jnp.stack([x0 * cos - x1 * sin, x0 * sin + x1 * cos], axis=-1)
            rotated = rotated.reshape(b, s, h, dim_half)
            return jnp.concatenate([rotated, x[..., dim_half:]], axis=-1)
        key = jax.random.key(seed)
        k0, k1, k2, k3, k4 = jax.random.split(key, 5)
        std = 0.02
        return {'hidden_states': jax.random.normal(k0, (B, S, HIDDEN), dtype=jnp.float32), 'Wq': jax.random.normal(k1, (HIDDEN, N_HEADS * HEAD_DIM), dtype=jnp.float32) * std, 'Wk': jax.random.normal(k2, (HIDDEN, N_KV_HEADS * HEAD_DIM), dtype=jnp.float32) * std, 'Wv': jax.random.normal(k3, (HIDDEN, N_KV_HEADS * HEAD_DIM), dtype=jnp.float32) * std, 'Wo': jax.random.normal(k4, (HIDDEN, HIDDEN), dtype=jnp.float32) * std}
    _L0_attn_in = _L0_attn_setup()

    def _L0_ffn_setup():
        import jax, jax.numpy as jnp
        import numpy as np
        EPS = 1e-08

        def _quantize(w):
            gamma = jnp.mean(jnp.abs(w))
            return jnp.clip(jnp.round(w / (gamma + EPS)), -1.0, 1.0)

        def _bitlinear(x, w):
            return jnp.matmul(x, _quantize(w).T)
        key = jax.random.key(seed)
        k1, k2, k3, k4 = jax.random.split(key, 4)
        d, h = (256, 704)
        x = jax.random.normal(k1, (4, 256, d), dtype=jnp.float32)
        w1 = jax.random.normal(k2, (h, d), dtype=jnp.float32)
        w2 = jax.random.normal(k3, (h, d), dtype=jnp.float32)
        w3 = jax.random.normal(k4, (d, h), dtype=jnp.float32)
        return {'x': x, 'w1': w1, 'w2': w2, 'w3': w3}
    _L0_ffn_in = _L0_ffn_setup()

    def _L1_attn_setup():
        import jax, jax.numpy as jnp
        import numpy as np
        H = 32
        KV = 8
        D = 64
        WIN = 64
        BASE = 10000.0

        def _rope_tables(S):
            inv_freq = 1.0 / BASE ** (jnp.arange(0, D, 2, dtype=jnp.float32) / D)
            t = jnp.arange(S, dtype=jnp.float32)
            freqs = t[:, None] * inv_freq[None, :]
            emb = jnp.concatenate([freqs, freqs], axis=-1)
            return (jnp.cos(emb)[:, None, :], jnp.sin(emb)[:, None, :])

        def _rotate_half(u):
            return jnp.concatenate([-u[..., D // 2:], u[..., :D // 2]], axis=-1)
        key = jax.random.key(seed)
        ks = jax.random.split(key, 5)
        B, S, DIM = (2, 256, 256)
        x = jax.random.normal(ks[0], (B, S, DIM), dtype=jnp.float32)
        wq = jax.random.normal(ks[1], (H * D, DIM), dtype=jnp.float32) * 0.02
        wk = jax.random.normal(ks[2], (KV * D, DIM), dtype=jnp.float32) * 0.02
        wv = jax.random.normal(ks[3], (KV * D, DIM), dtype=jnp.float32) * 0.02
        wo = jax.random.normal(ks[4], (DIM, H * D), dtype=jnp.float32) * 0.02
        return {'x': x, 'wq': wq, 'wk': wk, 'wv': wv, 'wo': wo}
    _L1_attn_in = _L1_attn_setup()

    def _L1_ffn_setup():
        import jax, jax.numpy as jnp
        import numpy as np
        D_MODEL = 256
        D_FF = 1024

        def absmean_quant(w):
            scale = jnp.mean(jnp.abs(w))
            mask = (jnp.abs(w) >= scale * 0.7).astype(w.dtype)
            return jnp.sign(w) * mask
        key = jax.random.key(seed)
        k_x, k_w1, k_w2 = jax.random.split(key, 3)
        x = jax.random.normal(k_x, (4, 512, D_MODEL), dtype=jnp.float32)
        w1 = jax.random.normal(k_w1, (D_FF, D_MODEL), dtype=jnp.float32)
        b1 = jnp.zeros((D_FF,), dtype=jnp.float32)
        w2 = jax.random.normal(k_w2, (D_MODEL, D_FF), dtype=jnp.float32)
        b2 = jnp.zeros((D_MODEL,), dtype=jnp.float32)
        return {'x': x, 'w1': w1, 'b1': b1, 'w2': w2, 'b2': b2}
    _L1_ffn_in = _L1_ffn_setup()
    _d = {'L0_attn_hidden_states': _L0_attn_in['hidden_states'], 'L0_attn_Wq': _L0_attn_in['Wq'], 'L0_attn_Wk': _L0_attn_in['Wk'], 'L0_attn_Wv': _L0_attn_in['Wv'], 'L0_attn_Wo': _L0_attn_in['Wo'], 'L0_ffn_w1': _L0_ffn_in['w1'], 'L0_ffn_w2': _L0_ffn_in['w2'], 'L0_ffn_w3': _L0_ffn_in['w3'], 'L1_attn_wq': _L1_attn_in['wq'], 'L1_attn_wk': _L1_attn_in['wk'], 'L1_attn_wv': _L1_attn_in['wv'], 'L1_attn_wo': _L1_attn_in['wo'], 'L1_ffn_w1': _L1_ffn_in['w1'], 'L1_ffn_b1': _L1_ffn_in['b1'], 'L1_ffn_w2': _L1_ffn_in['w2'], 'L1_ffn_b2': _L1_ffn_in['b2']}
    _x0 = _d['L0_attn_hidden_states']
    _d['L0_attn_hidden_states'] = jax.random.normal(jax.random.fold_in(jax.random.key(seed), 1), (2, 1024, 256), dtype=_x0.dtype)
    del _x0
    return _d

def reference(L0_attn_hidden_states, L0_attn_Wq, L0_attn_Wk, L0_attn_Wv, L0_attn_Wo, L0_ffn_w1, L0_ffn_w2, L0_ffn_w3, L1_attn_wq, L1_attn_wk, L1_attn_wv, L1_attn_wo, L1_ffn_w1, L1_ffn_b1, L1_ffn_w2, L1_ffn_b2):

    def _L0_attn_ref(hidden_states, Wq, Wk, Wv, Wo):
        import jax, jax.numpy as jnp
        import numpy as np
        HIDDEN = 256
        N_HEADS = 16
        N_KV_HEADS = 4
        HEAD_DIM = HIDDEN // N_HEADS
        ROPE_THETA = 10000.0
        B, S = (1, 256)

        def _apply_rope(x, position_ids, theta=ROPE_THETA):
            b, s, h, hd = x.shape
            dim_half = hd // 2
            inv_freq = 1.0 / theta ** (jnp.arange(0, dim_half, 2, dtype=jnp.float32) / dim_half)
            freqs = position_ids[:, :, None].astype(jnp.float32) * inv_freq[None, None, :]
            cos = jnp.cos(freqs)[:, :, None, :]
            sin = jnp.sin(freqs)[:, :, None, :]
            x_rot = x[..., :dim_half].reshape(b, s, h, dim_half // 2, 2)
            x0, x1 = (x_rot[..., 0], x_rot[..., 1])
            rotated = jnp.stack([x0 * cos - x1 * sin, x0 * sin + x1 * cos], axis=-1)
            rotated = rotated.reshape(b, s, h, dim_half)
            return jnp.concatenate([rotated, x[..., dim_half:]], axis=-1)
        b, s, _ = hidden_states.shape
        groups = N_HEADS // N_KV_HEADS
        q = (hidden_states @ Wq).reshape(b, s, N_HEADS, HEAD_DIM)
        k = (hidden_states @ Wk).reshape(b, s, N_KV_HEADS, HEAD_DIM)
        v = (hidden_states @ Wv).reshape(b, s, N_KV_HEADS, HEAD_DIM)
        position_ids = jnp.broadcast_to(jnp.arange(s)[None, :], (b, s))
        q = _apply_rope(q, position_ids)
        k = _apply_rope(k, position_ids)
        if groups > 1:
            k = jnp.repeat(k, groups, axis=2)
            v = jnp.repeat(v, groups, axis=2)
        scale = 1.0 / jnp.sqrt(jnp.float32(HEAD_DIM))
        scores = jnp.einsum('bshd,bthd->bhst', q, k) * scale
        attn = jax.nn.softmax(scores, axis=-1)
        out = jnp.einsum('bhst,bthd->bshd', attn, v)
        out = out.reshape(b, s, HIDDEN)
        return out @ Wo

    def _L0_ffn_ref(x, w1, w2, w3):
        import jax, jax.numpy as jnp
        import numpy as np
        EPS = 1e-08

        def _quantize(w):
            gamma = jnp.mean(jnp.abs(w))
            return jnp.clip(jnp.round(w / (gamma + EPS)), -1.0, 1.0)

        def _bitlinear(x, w):
            return jnp.matmul(x, _quantize(w).T)
        x1 = _bitlinear(x, w1)
        x2 = _bitlinear(x, w2)
        hidden = jax.nn.sigmoid(x1) * x2
        return _bitlinear(hidden, w3)

    def _L1_attn_ref(x, wq, wk, wv, wo):
        import jax, jax.numpy as jnp
        import numpy as np
        H = 32
        KV = 8
        D = 64
        WIN = 64
        BASE = 10000.0

        def _rope_tables(S):
            inv_freq = 1.0 / BASE ** (jnp.arange(0, D, 2, dtype=jnp.float32) / D)
            t = jnp.arange(S, dtype=jnp.float32)
            freqs = t[:, None] * inv_freq[None, :]
            emb = jnp.concatenate([freqs, freqs], axis=-1)
            return (jnp.cos(emb)[:, None, :], jnp.sin(emb)[:, None, :])

        def _rotate_half(u):
            return jnp.concatenate([-u[..., D // 2:], u[..., :D // 2]], axis=-1)
        B, S, _ = x.shape
        q = (x @ wq.T).reshape(B, S, H, D)
        k = (x @ wk.T).reshape(B, S, KV, D)
        v = (x @ wv.T).reshape(B, S, KV, D)
        cos, sin = _rope_tables(S)
        q = q * cos + _rotate_half(q) * sin
        k = k * cos + _rotate_half(k) * sin
        q = q.transpose(0, 2, 1, 3)
        k = jnp.repeat(k.transpose(0, 2, 1, 3), H // KV, axis=1)
        v = jnp.repeat(v.transpose(0, 2, 1, 3), H // KV, axis=1)
        scale = 1.0 / jnp.sqrt(jnp.float32(D))
        scores = jnp.einsum('bhqd,bhkd->bhqk', q, k) * scale
        i = jnp.arange(S)[:, None]
        j = jnp.arange(S)[None, :]
        window_mask = jnp.abs(i - j) > WIN // 2
        causal_mask = j > i
        masked = window_mask | causal_mask
        scores = jnp.where(masked[None, None], -jnp.inf, scores)
        attn = jax.nn.softmax(scores, axis=-1)
        out = jnp.einsum('bhqk,bhkd->bhqd', attn, v)
        out = out.transpose(0, 2, 1, 3).reshape(B, S, H * D)
        return out @ wo.T

    def _L1_ffn_ref(x, w1, b1, w2, b2):
        import jax, jax.numpy as jnp
        import numpy as np
        D_MODEL = 256
        D_FF = 1024

        def absmean_quant(w):
            scale = jnp.mean(jnp.abs(w))
            mask = (jnp.abs(w) >= scale * 0.7).astype(w.dtype)
            return jnp.sign(w) * mask
        w1_q = absmean_quant(w1)
        w2_q = absmean_quant(w2)
        h = jnp.einsum('bsd,fd->bsf', x, w1_q) + b1
        h = jax.nn.gelu(h, approximate=False)
        out = jnp.einsum('bsf,df->bsd', h, w2_q) + b2
        return out
    x = L0_attn_hidden_states
    x = x + _L0_attn_ref(_layernorm(x, axis=-1), L0_attn_Wq, L0_attn_Wk, L0_attn_Wv, L0_attn_Wo)
    x = x + _L0_ffn_ref(_layernorm(x, axis=-1), L0_ffn_w1, L0_ffn_w2, L0_ffn_w3)
    x = x + _L1_attn_ref(_layernorm(x, axis=-1), L1_attn_wq, L1_attn_wk, L1_attn_wv, L1_attn_wo)
    x = x + _L1_ffn_ref(_layernorm(x, axis=-1), L1_ffn_w1, L1_ffn_b1, L1_ffn_w2, L1_ffn_b2)
    return x

_drawn_inputs = setup_inputs


def setup_inputs(seed=0):
    import zlib

    import numpy as np

    out = dict(_drawn_inputs(seed))
    spreads = {'L1_ffn_b1': (0.0, 0.8), 'L1_ffn_b2': (0.0, 0.8)}
    factors = {'L0_attn_Wq': 8.0,
     'L0_attn_Wk': 8.0,
     'L0_attn_Wv': 8.0,
     'L0_attn_Wo': 8.0,
     'L1_attn_wq': 8.0,
     'L1_attn_wk': 8.0,
     'L1_attn_wv': 8.0,
     'L1_attn_wo': 8.0}
    for name, (base, spread) in spreads.items():
        noise = np.random.default_rng([zlib.crc32(name.encode()), seed]).standard_normal(out[name].shape)
        drawn = base * np.exp(spread * noise) if base else spread * noise
        out[name] = jnp.asarray(drawn.astype(out[name].dtype))
    for name, factor in factors.items():
        out[name] = (out[name] * factor).astype(out[name].dtype)
    return out
```

```python
from contextlib import ExitStack

import numpy as np

import concourse.bass as bass
from concourse import mybir

F32 = mybir.dt.float32
F16 = mybir.dt.float16
ALU = mybir.AluOpType
ACT = mybir.ActivationFunctionType
AX = mybir.AxisListType

P = 128
B, S, DM = 2, 1024, 256
NT = S // P
KC = DM // P
EPS = 1e-5
H0, KV0, D0 = 16, 4, 16
G0 = H0 // KV0
HD0 = H0 + KV0
QKV0 = (H0 + 2 * KV0) * D0
F0 = 704
FC0 = [P] * (F0 // P) + [F0 % P]
H1, KV1, D1, WIN = 32, 8, 64, 32
G1 = H1 // KV1
QB = 32
NQB = P // QB
GP1 = KV1 // 2
F1 = 1024
FC1 = [P] * (F1 // P)
MASKED = -60000.0
HALF = 512


def build(nc, x_in, cos0, sin0, cos1, sin1, ident, mask, wqkv0, wo0, w1, w2, w3,
          wq1, wk1, wv1, wo1, f1w1, f1b1, f1w2, f1b2, out):
    ctx = ExitStack()
    with ctx:
        def sb(name, shape, dt=F32):
            return ctx.enter_context(nc.sbuf_tensor(name, shape, dt))

        def sem(name):
            return ctx.enter_context(nc.semaphore(name))

        psum = ctx.enter_context(nc.psum_tensor("psum", [P, 8, HALF], F32))

        def bank(i):
            return psum[:, i, :]

        def bank16(i):
            return psum[:, i, :].bitcast(F16)

        id32 = sb("id32", [P, P])
        id16 = sb("id16", [P, P], F16)
        ones = sb("ones", [P, P])
        mask16 = sb("mask16", [P, 2, HALF], F16)
        c0 = sb("c0", [P, NT, 8])
        s0 = sb("s0", [P, NT, 8])
        c1 = sb("c1", [P, NT, 32])
        s1 = sb("s1", [P, NT, 2, 32])
        wqkv0_s = sb("wqkv0_s", [P, KC, QKV0])
        wo0_s = sb("wo0_s", [P, KC, DM])
        wq1_s = sb("wq1_s", [P, KC, H1 * D1])
        wk1_s = sb("wk1_s", [P, KC, KV1 * D1])
        wv1_s = sb("wv1_s", [P, KC, KV1 * D1])
        wo1_s = sb("wo1_s", [P, H1 * D1 // P, DM])
        t1 = sb("t1", [P, KC, F0], F16)
        t2 = sb("t2", [P, KC, F0], F16)
        t3 = sb("t3", [P, len(FC0), DM], F16)
        u1 = sb("u1", [P, KC, F1], F16)
        u2 = sb("u2", [P, len(FC1), DM], F16)
        b1c = sb("b1c", [P, len(FC1)])
        b2r = sb("b2r", [P, DM])
        wabs = sb("wabs", [P, 8])
        thr = sb("thr", [P, 3, 5])
        x = sb("x", [P, NT, DM])
        stats = sb("stats", [P, NT, 6])
        mv = sb("mv", [P, NT, 2])
        rstd = sb("rstd", [P, NT])
        mhalf = sb("mhalf", [P, 1])
        xn = sb("xn", [P, NT, DM])
        xnT = sb("xnT", [P, KC, S])
        otok = sb("otok", [P, NT, DM])

        REGION = 100 * 1024 // 4
        region = sb("region", [P, REGION])
        cut = [0]

        def share(cols, dt=F32):
            words = cols if dt == F32 else cols // 2
            a = region[:, cut[0]:cut[0] + words]
            cut[0] += words
            assert cut[0] <= REGION, cut[0]
            return a if dt == F32 else a.bitcast(dt)

        raw1 = share(KC * F0).rearrange("p (k f) -> p k f", k=KC)
        raw2 = share(KC * F0).rearrange("p (k f) -> p k f", k=KC)
        raw3 = share(len(FC0) * DM).rearrange("p (k f) -> p k f", k=len(FC0))
        raw4 = share(KC * F1).rearrange("p (k f) -> p k f", k=KC)
        raw5 = share(len(FC1) * DM).rearrange("p (k f) -> p k f", k=len(FC1))
        neg16 = share(2048, F16)
        cut[0] = 0
        QT = share(H0 * S, F16).rearrange("p (h s) -> p h s", h=H0)
        KT = share(KV0 * S, F16).rearrange("p (h s) -> p h s", h=KV0)
        V0 = share(NT * KV0 * 32).rearrange("p (t g d) -> p t g d", t=NT, g=KV0)
        PR = 8
        prob0 = share(PR * HALF).rearrange("p (r n) -> p r n", r=PR)
        osum = share(HALF)
        orec = share(NQB * G0)
        mneg = share(2 * G0 * NT, F16).rearrange("p (r n) -> p r n", r=2)
        qk32 = share(2 * HD0 * D0).rearrange("p (r h d) -> p r h d", r=2, h=HD0)
        ropeA = share(HD0 * 8).rearrange("p (h d) -> p h d", h=HD0)
        ropeB = share(HD0 * 8).rearrange("p (h d) -> p h d", h=HD0)
        TW = 66
        T16 = share(2 * HD0 * TW, F16).rearrange("p (r h d) -> p r h d", r=2, h=HD0)
        cut[0] = 0
        xhi = share(KC * S, F16).rearrange("p (k s) -> p k s", k=KC)
        xlo = share(KC * S, F16).rearrange("p (k s) -> p k s", k=KC)
        NFR = 4
        gate = share(NFR * HALF).rearrange("p (r n) -> p r n", r=NFR)
        hid = share(NFR * HALF).rearrange("p (r n) -> p r n", r=NFR)
        hhi = share(16 * HALF, F16).rearrange("p (f n) -> p f n", f=16)
        hlo = share(16 * HALF, F16).rearrange("p (f n) -> p f n", f=16)
        oT = share(2 * DM).rearrange("p (r n) -> p r n", r=2)
        cut[0] = 0
        NR = KV1 * D1
        NPC = (H1 + KV1) * D1 // NR
        rA = share(2 * NR).rearrange("p (r n) -> p r n", r=2)
        rB = share(2 * NR).rearrange("p (r n) -> p r n", r=2)
        rot = share(2 * NR).rearrange("p (r n) -> p r n", r=2)
        QT1 = share(16 * P).rearrange("p (c s) -> p c s", c=16)
        KR = 3
        Kz = share(GP1 * 2 * KR * P).rearrange("p (g e r s) -> p g e r s", g=GP1, e=2, r=KR)
        VR = 4
        Vb = share(VR * NQB * GP1 * P).rearrange("p (r q g d) -> p r q g d", r=VR, q=NQB, g=GP1)
        sT = share(2 * HALF).rearrange("p (r n) -> p r n", r=2)
        sE = share(2 * HALF).rearrange("p (r n) -> p r n", r=2)
        smax = share(2 * 8).rearrange("p (r n) -> p r n", r=2)
        ssum = share(2 * 8).rearrange("p (r n) -> p r n", r=2)
        PT = share(2 * NQB * 256).rearrange("p (s q n) -> p s q n", s=2, q=NQB)
        OT1 = share(GP1 * G1 * P).rearrange("p (g h s) -> p g h s", g=GP1, h=G1)

        loaded = sem("loaded")
        consts = sem("consts")
        absdone = sem("absdone")
        absall = sem("absall")
        thrdone = sem("thrdone")
        negdone = sem("negdone")
        quant = sem("quant")
        dconst = sem("dconst")
        qstep = sem("qstep")
        cleared = {e: sem(f"cleared_{e}") for e in ("pe", "act", "dve", "sp")}
        row_end = sem("row_end")
        x_loaded = sem("x_loaded")
        x_stored = sem("x_stored")
        phase_end = {e: sem(f"phase_end_{e}") for e in ("pe", "act", "dve", "pool")}
        stat_done = sem("stat_done")
        var_ready = sem("var_ready")
        eps_added = sem("eps_added")
        rstd_ready = sem("rstd_ready")
        xn_ready = sem("xn_ready")
        xn_moved = sem("xn_moved")
        xT_ready = sem("xT_ready")
        x_res = sem("x_res")
        qkv_ready = sem("qkv_ready")
        v0_out = sem("v0_out")
        rope_mul = sem("rope_mul")
        rope_done = sem("rope_done")
        hi_done = sem("hi_done")
        lo_done = sem("lo_done")
        hT_ready = sem("hT_ready")
        hT_dve = sem("hT_dve")
        hT_act = sem("hT_act")
        prep = sem("prep")
        prep4 = sem("prep4")
        max_ready = sem("max_ready")
        max_done = sem("max_done")
        mrow_ready = sem("mrow_ready")
        mrow_moved = sem("mrow_moved")
        st_ready = sem("st_ready")
        exp_done = sem("exp_done")
        pv_done = sem("pv_done")
        osum_done = sem("osum_done")
        oTr_ready = sem("oTr_ready")
        orec_done = sem("orec_done")
        o_done = sem("o_done")
        ot_ready = sem("ot_ready")
        ot_moved = sem("ot_moved")
        wo_ready = sem("wo_ready")
        hi2_done = sem("hi2_done")
        lo2_done = sem("lo2_done")
        up_ready = sem("up_ready")
        gate_done = sem("gate_done")
        hid_done = sem("hid_done")
        hhi_done = sem("hhi_done")
        hlo_done = sem("hlo_done")
        down_ready = sem("down_ready")
        b2_done = sem("b2_done")
        pj_ready = sem("pj_ready")
        pj_read = sem("pj_read")
        pj_rot = sem("pj_rot")
        tr_ready = sem("tr_ready")
        tr_moved = sem("tr_moved")
        vp_ready = sem("vp_ready")
        vp_moved = sem("vp_moved")
        sc_ready = sem("sc_ready")
        sT_done = sem("sT_done")
        mx_done = sem("mx_done")
        sub_done = sem("sub_done")
        ex_done = sem("ex_done")
        sm_done = sem("sm_done")
        rc_done = sem("rc_done")
        nrm_done = sem("nrm_done")
        pT_done = sem("pT_done")
        pv1_ready = sem("pv1_ready")
        pv1_moved = sem("pv1_moved")

        row_sems = range(row_end.num, pv1_moved.num + 1)

        def at(b, per, n):
            assert 0 <= n <= per, (n, per)
            return n

        PH = 5
        NLOAD = 20
        names = ("pe", "act", "dve", "pool")

        def enter(e, me, b, ph):
            for other in names:
                if other != me and ph > 0:
                    e.wait_ge(phase_end[other], at(b, PH, ph))

        def end_row(e, me):
            e.drain().then_inc(row_end, 1)
            e.wait_ge(cleared[me], 1)
            e.sem_clear(cleared[me])

        def leave(e, me):
            e.drain().then_inc(phase_end[me], 1)

        block = ctx.enter_context(nc.Block())
        dve, act, pe, pool, sp = nc.vector, nc.scalar, nc.tensor, nc.gpsimd, nc.sync

        XR = 32

        def ln_stats(e, b, use, t, after_res):
            if after_res:
                e.wait_ge(x_res, at(b, XR, after_res))
            dve.bn_stats(stats[:, t, :], x[:, t, :]).then_inc(stat_done, 1)
            e.wait_ge(stat_done, at(b, 32, 8 * use + t + 1))
            dve.bn_aggr(mv[:, t, :], stats[:, t, :]).then_inc(var_ready, 1)

        def ln_norm(e, b, use, t):
            i = 8 * use + t
            e.wait_ge(rstd_ready, at(b, 32, i + 1))
            if i >= 8:
                e.wait_ge(xn_moved, at(b, 32, i - 7))
            dve.tensor_scalar(xn[:, t, :], x[:, t, :], mv[:, t, 0:1], rstd[:, t:t + 1],
                              ALU.subtract, ALU.mult).then_inc(xn_ready, 1)

        def ln_pow(e, b, use, t):
            i = 8 * use + t
            e.wait_ge(var_ready, at(b, 32, i + 1))
            pool.tensor_scalar(rstd[:, t:t + 1], mv[:, t, 1:2], EPS, None, ALU.add).then_inc(eps_added, 1)
            e.wait_ge(eps_added, at(b, 32, i + 1))
            pool.tensor_tensor(rstd[:, t:t + 1], rstd[:, t:t + 1], mhalf[:], ALU.pow).then_inc(rstd_ready, 1)

        def transpose_tile(e, b, use, t, dst, ready=None):
            i = 8 * use + t
            e.wait_ge(xn_ready, at(b, 32, i + 1))
            for k in range(KC):
                last = pe.transpose(dst[:, k, :], xn[:, t, k * P:(k + 1) * P], id32[:])
            last.then_inc(xn_moved, 1)

        def stat_kind(kind_list, n):
            return sum(1 for k in kind_list[:n + 1] if k == kind_list[n])

        NHG = 2 * KV0
        NK = S // P
        spread = [3, 2, 2, 3, 2, 2, 2, 0]
        slots, plan = ["max"] * 16 + ["row"], []
        first_slots = len(slots)
        for j in range(NHG):
            row = []
            for kt in range(NK):
                todo = []
                if j + 1 < NHG:
                    todo += ["max"] * spread[kt]
                if kt == 1 and j >= 1:
                    todo += ["out"]
                if kt == NK - 1 and j + 1 < NHG:
                    todo += ["row"]
                row.append((len(slots), todo))
                slots += todo
            plan.append(row)
        slots.append("out")
        nth = [stat_kind(slots, n) for n in range(len(slots))]
        PV_LAG = 1

        def ffn_sizes(layer):
            return FC0 if layer == 0 else FC1

        def up_base(layer):
            return 0 if layer == 0 else 2 * len(FC0)

        NUP = 2 * len(FC0) + 2 * len(FC1)

        tr_plan = [("x", 0)]
        steps = []
        for s in range(NT + 2):
            st = []
            for i in range(NPC):
                n = NPC * s + i
                group = []
                if 2 <= n < NPC * NT + 2:
                    group.append((len(tr_plan), "q", n - 2))
                    tr_plan.append(("q", n - 2))
                if i == 3 and s + 1 < NT:
                    group.append((len(tr_plan), "x", s + 1))
                    tr_plan.append(("x", s + 1))
                st.append(group)
            steps.append(st)
        NTR = len(tr_plan)

        def ffn_pe(e, b, layer):
            MM = pe.matmul
            sizes = ffn_sizes(layer)
            nf = len(sizes)
            base = up_base(layer)
            use = 1 if layer == 0 else 3

            def turn_chunk(c):
                if c == 1:
                    e.wait_ge(lo2_done, at(b, 8, 4 * layer + 2))
                view = psum[:, 0:2, :]
                for i in range(4):
                    transpose_tile(e, b, use, 4 * c + i, view[:, :, i * P:(i + 1) * P])

            def up(c):
                if c == 0:
                    e.wait_ge(lo2_done, at(b, 8, 4 * layer + 2))
                else:
                    e.wait_ge(lo2_done, at(b, 8, 4 * layer + 4))
                for f, size in enumerate(sizes):
                    n = c * nf + f
                    if layer == 0:
                        if n >= 2:
                            e.wait_ge(gate_done, at(b, NUP, base + n - 1))
                            e.wait_ge(hid_done, at(b, 12, n - 1))
                        outs = ((t1, bank(2 + n % 2)), (t2, bank(4 + n % 2)))
                    else:
                        if n >= 4:
                            e.wait_ge(gate_done, at(b, NUP, base + n - 3))
                        outs = ((u1, bank(2 + n % 4)),)
                    for w, o in outs:
                        for k in range(KC):
                            for part, xs in enumerate((xhi, xlo)):
                                last = MM(o[0:size, :], w[:, k, f * P:f * P + size], xs[:, k, c * HALF:(c + 1) * HALF],
                                          start=(k == 0 and part == 0), stop=(k == KC - 1 and part == 1))
                    last.then_inc(up_ready, 1)

            def down(c):
                w = t3 if layer == 0 else u2
                for i in range(4):
                    m = 4 * c + i
                    if m >= 2:
                        e.wait_ge(x_res, at(b, XR, (8 if layer == 0 else 24) + m - 1))
                    for f, size in enumerate(sizes):
                        if i == 0:
                            e.wait_ge(hlo_done, at(b, NUP, base + c * nf + f + 1))
                        for part, hs in enumerate((hhi, hlo)):
                            last = MM(bank(6 + m % 2)[:, 0:DM], hs[0:size, 8 * c + f, i * P:(i + 1) * P], w[0:size, f, :],
                                      start=(f == 0 and part == 0), stop=(f == nf - 1 and part == 1))
                    last.then_inc(down_ready, 1)

            turn_chunk(0)
            up(0)
            turn_chunk(1)
            up(1)
            down(0)
            down(1)

        def slot_of(kind, j):
            return [n for n in range(len(slots)) if slots[n] == kind][j]

        def ffn_act(e, b, layer):
            sizes = ffn_sizes(layer)
            nf = len(sizes)
            base = up_base(layer)
            for c in range(2):
                e.wait_ge(xn_moved, at(b, 32, (8 if layer == 0 else 24) + 4 * (c + 1)))
                for k in range(KC):
                    act.copy(xhi[:, k, c * HALF:(c + 1) * HALF], bank(k)).then_inc(hi2_done, 1)
                for f, size in enumerate(sizes):
                    n = c * nf + f
                    e.wait_ge(up_ready, at(b, NUP, base + n + 1))
                    if layer == 0:
                        if n >= NFR:
                            e.wait_ge(hid_done, at(b, 12, n - NFR + 1))
                        act.activation(gate[0:size, n % NFR, :], bank(2 + n % 2)[0:size, :], ACT.Sigmoid).then_inc(gate_done, 1)
                    else:
                        if n >= NFR:
                            e.wait_ge(hlo_done, at(b, NUP, base + n - NFR + 1))
                        act.activation(hid[0:size, n % NFR, :], bank(2 + n % 4)[0:size, :], ACT.Gelu,
                                       bias=b1c[:, f:f + 1]).then_inc(gate_done, 1)

        def ffn_dve(e, b, layer):
            sizes = ffn_sizes(layer)
            nf = len(sizes)
            base = up_base(layer)

            def low(n):
                c, f = n // nf, n % nf
                size = sizes[f]
                e.wait_ge(hid_done if layer == 0 else gate_done,
                          at(b, 12 if layer == 0 else NUP, n + 1 if layer == 0 else base + n + 1))
                dve.tensor_copy(hhi[0:size, 8 * c + f, :], hid[0:size, n % NFR, :]).then_inc(hhi_done, 1)
                e.wait_ge(hhi_done, at(b, NUP, base + n + 1))
                dve.tensor_tensor(hlo[0:size, 8 * c + f, :], hid[0:size, n % NFR, :], hhi[0:size, 8 * c + f, :],
                                  ALU.subtract).then_inc(hlo_done, 1)

            for c in range(2):
                for k in range(KC):
                    e.wait_ge(hi2_done, at(b, 8, 4 * layer + 2 * c + k + 1))
                    dve.tensor_tensor(xlo[:, k, c * HALF:(c + 1) * HALF], bank(k), xhi[:, k, c * HALF:(c + 1) * HALF],
                                      ALU.subtract).then_inc(lo2_done, 1)
                for f, size in enumerate(sizes):
                    n = c * nf + f
                    if layer == 0:
                        e.wait_ge(gate_done, at(b, NUP, base + n + 1))
                        if n >= NFR:
                            e.wait_ge(hlo_done, at(b, NUP, base + n - NFR + 1))
                        dve.tensor_tensor(hid[0:size, n % NFR, :], bank(4 + n % 2)[0:size, :], gate[0:size, n % NFR, :],
                                          ALU.mult).then_inc(hid_done, 1)
                    if n >= 1:
                        low(n - 1)
            low(2 * nf - 1)
            for t in range(NT):
                done = (8 if layer == 0 else 24) + t
                e.wait_ge(down_ready, at(b, 2 * NT, NT * layer + t + 1))
                if layer == 1:
                    e.wait_ge(b2_done, at(b, NT, t + 1))
                dve.tensor_tensor(x[:, t, :], bank(6 + t % 2)[:, 0:DM], x[:, t, :], ALU.add).then_inc(x_res, 1)
                if layer == 0:
                    ln_stats(e, b, 2, t, done + 1)
                    if t >= 1:
                        ln_norm(e, b, 2, t - 1)
            if layer == 0:
                ln_norm(e, b, 2, NT - 1)

        def ffn_pool(e, b, layer):
            if layer == 1:
                for t in range(NT):
                    e.wait_ge(xn_ready, at(b, 32, 24 + t + 1))
                    pool.tensor_tensor(x[:, t, :], x[:, t, :], b2r[:], ALU.add).then_inc(b2_done, 1)
        @block.sync
        def _(e):
            for dst, src in (
                    (raw1, w1.rearrange("(k p) f -> p k f", p=P)),
                    (raw2, w2.rearrange("(k p) f -> p k f", p=P)),
                    (raw3[:, 0:5, :], w3[0:640, :].rearrange("(k p) f -> p k f", p=P)),
                    (raw3[0:64, 5, :], w3[640:704, :]),
                    (raw4, f1w1.rearrange("(k p) f -> p k f", p=P)),
                    (raw5, f1w2.rearrange("(k p) f -> p k f", p=P)),
                    (id32[:], ident),
                    (c0[:], cos0.rearrange("(t p) c -> p t c", p=P)),
                    (s0[:], sin0.rearrange("(t p) c -> p t c", p=P)),
                    (c1[:], cos1.rearrange("(t p) c -> p t c", p=P)),
                    (s1[:].rearrange("p t a c -> p t (a c)"), sin1.rearrange("(t p) c -> p t c", p=P)),
                    (mask16[:].rearrange("p a n -> p (a n)"), mask),
                    (wqkv0_s[:], wqkv0.rearrange("(k p) f -> p k f", p=P)),
                    (wo0_s[:], wo0.rearrange("(k p) f -> p k f", p=P)),
                    (wk1_s[:], wk1.rearrange("(k p) f -> p k f", p=P)),
                    (wv1_s[:], wv1.rearrange("(k p) f -> p k f", p=P)),
                    (wq1_s[:], wq1.rearrange("(k p) f -> p k f", p=P)),
                    (wo1_s[:], wo1.rearrange("(k p) f -> p k f", p=P)),
                    (b1c[:], f1b1),
                    (b2r[:], f1b2.rearrange("(a n) -> a n", a=1).to_broadcast([P, DM]))):
                e.dma_start(dst, src).then_inc(loaded, 16)
            with e.Fori(0, B) as b:
                e.dma_start(x[:], x_in[b, :, :].rearrange("(t p) d -> p t d", p=P)).then_inc(x_loaded, 16)
                e.wait_ge(x_res, at(b, XR, XR))
                e.dma_start(out[b, :, :].rearrange("(t p) d -> p t d", p=P), x[:]).then_inc(x_stored, 16)
                e.wait_ge(x_stored, at(b, 16, 16))
                end_row(e, "sp")

        @block.tensor
        def _(e):
            MM = pe.matmul
            e.wait_ge(consts, 1)
            e.wait_ge(absdone, 5)
            MM(bank(0)[:, 0:5], ones[:], wabs[:, 0:5], start=True, stop=True).then_inc(absall, 1)
            e.wait_ge(loaded, 16 * NLOAD)
            e.wait_ge(consts, 4)
            e.wait_ge(quant, 5)
            with e.Fori(0, B) as b:
                enter(e, "pe", b, 0)
                for t in range(NT + 3):
                    if t < NT:
                        if t >= 2:
                            e.wait_ge(xT_ready, at(b, 16, t - 1))
                        transpose_tile(e, b, 0, t, bank(t % 2)[:, 0:2 * P].rearrange("p (k s) -> p k s", k=KC))
                    u = t - 1
                    if 0 <= u < NT:
                        e.wait_ge(xT_ready, at(b, 16, u + 1))
                        if u >= 2:
                            e.wait_ge(rope_mul, at(b, NT, u - 1))
                            e.wait_ge(v0_out, at(b, NT, u - 1))
                        for k in range(KC):
                            last = MM(bank(2 + u % 2)[:, 0:QKV0], xnT[:, k, u * P:(u + 1) * P], wqkv0_s[:, k, :],
                                      start=(k == 0), stop=(k == KC - 1))
                        last.then_inc(qkv_ready, 1)
                    u = t - 3
                    if 0 <= u < NT:
                        e.wait_ge(lo_done, at(b, NT, u + 1))
                        for c, (h0, h1) in enumerate(((0, 8), (8, 16), (16, 20))):
                            if u >= 1:
                                if c == 1:
                                    e.wait_ge(hT_act, at(b, NT, u))
                                else:
                                    e.wait_ge(hT_dve, at(b, 2 * NT, 2 * u - 1 + c // 2))
                            for h in range(h0, h1):
                                last = pe.transpose(bank16(4 + c)[0:65, (h - h0) * P:(h - h0 + 1) * P],
                                                    T16[:, u % 2, h, 0:65], id16[:])
                            last.then_inc(hT_ready, 1)
                leave(e, "pe")
                enter(e, "pe", b, 1)

                def slot(n, todo_j):
                    if n >= 2:
                        prev = {"max": (max_done, 16 * NHG), "row": (mrow_moved, NHG), "out": (o_done, NHG)}[slots[n - 2]]
                        e.wait_ge(prev[0], at(b, prev[1], nth[n - 2]))
                    pair = 2 * (n % 2)
                    if slots[n] == "max":
                        m = nth[n] - 1
                        j, h, qt = m // 16, m // 4 % 4, m % 4
                        kv, qc = j // 2, j % 2
                        for half in range(2):
                            last = MM(bank(pair + half), QT[:, 4 * kv + h, (4 * qc + qt) * P:(4 * qc + qt + 1) * P],
                                      KT[:, kv, half * HALF:(half + 1) * HALF], start=True, stop=True)
                        last.then_inc(max_ready, 1)
                    elif slots[n] == "row":
                        j = nth[n] - 1
                        e.wait_ge(max_done, at(b, 16 * NHG, 16 * (j + 1)))
                        dst = psum[64:65, pair:pair + 2, :].rearrange("p a n -> p (a n)").bitcast(F16)
                        for i in range(16):
                            last = pe.matmul(dst[:, i * P:(i + 1) * P], mneg[:, j % 2, i:i + 1], id16[:],
                                             start=True, stop=True, is_transpose=True, tile_position=(0, 64))
                        last.then_inc(mrow_ready, 1)
                    else:
                        j = nth[n] - 1
                        e.wait_ge(osum_done, at(b, NHG, j + 1))
                        for i in range(4):
                            last = pe.transpose(bank(pair)[:, i * P:(i + 1) * P], osum[:, i * P:(i + 1) * P], id32[:])
                        last.then_inc(oTr_ready, 1)

                def products(j, kt):
                    n0 = (j * NK + kt) * G0
                    if kt == 0 and j >= 1:
                        e.wait_ge(osum_done, at(b, NHG, j))
                    e.wait_ge(exp_done, at(b, 4 * NHG * NK, n0 + G0))
                    for h in range(G0):
                        last = MM(psum[32 * h:32 * h + 32, 7, :], V0[:, kt, j // 2, :], prob0[:, (n0 + h) % PR, :],
                                  start=(kt == 0), stop=(kt == NK - 1), tile_position=(0, 32 * h))
                    last.then_inc(pv_done, 1)

                for n in range(first_slots):
                    slot(n, 0)
                for j in range(NHG):
                    e.wait_ge(mrow_moved, at(b, NHG, j + 1))
                    for kt in range(NK):
                        n0 = (j * NK + kt) * G0
                        base, todo = plan[j][kt]
                        left = list(range(base, base + len(todo)))
                        if kt == NK - 1:
                            held, left = left, []
                        for h in range(G0):
                            n = n0 + h
                            if n >= 3:
                                e.wait_ge(exp_done, at(b, 4 * NHG * NK, n - 2))
                            MM(bank(4 + n % 3), KT[:, j // 2, kt * P:(kt + 1) * P],
                               QT[:, 4 * (j // 2) + h, (j % 2) * HALF:(j % 2 + 1) * HALF],
                               start=True, stop=True).then_inc(st_ready, 1)
                            if h % 2 == 1 and left:
                                slot(left.pop(0), j)
                        while left:
                            slot(left.pop(0), j)
                        if kt >= 1:
                            products(j, kt - 1)
                    for n in held:
                        slot(n, j)
                    products(j, NK - 1)
                slot(len(slots) - 1, NHG)
                leave(e, "pe")
                enter(e, "pe", b, 2)
                for t in range(NT + 1):
                    if t < NT:
                        if t >= 2:
                            e.wait_ge(ot_moved, at(b, NT, t - 1))
                        for k in range(KC):
                            last = pe.transpose(bank(t % 2)[:, k * P:(k + 1) * P], otok[:, t, k * P:(k + 1) * P], id32[:])
                        last.then_inc(ot_ready, 1)
                    u = t - 1
                    if u >= 0:
                        e.wait_ge(ot_moved, at(b, NT, u + 1))
                        if u >= 2:
                            e.wait_ge(x_res, at(b, XR, u - 1))
                        for k in range(KC):
                            last = MM(bank(2 + u % 2)[:, 0:DM], oT[:, u % 2, k * P:(k + 1) * P], wo0_s[:, k, :],
                                      start=(k == 0), stop=(k == KC - 1))
                        last.then_inc(wo_ready, 1)
                ffn_pe(e, b, 0)
                leave(e, "pe")
                enter(e, "pe", b, 3)

                def bank3(idx):
                    if idx >= 1:
                        e.wait_ge(tr_moved, at(b, NTR, idx))

                def turn(idx, kind, n):
                    bank3(idx)
                    if kind == "x":
                        transpose_tile(e, b, 2, n, bank(3)[:, 0:2 * P].rearrange("p (k s) -> p k s", k=KC))
                    else:
                        e.wait_ge(pj_rot, at(b, NPC * NT, n + 1))
                        for c in range(4):
                            last = pe.transpose(bank(3)[:, c * P:(c + 1) * P], rot[:, n % 2, c * P:(c + 1) * P], id32[:])
                        last.then_inc(tr_ready, 1)

                def project(n):
                    s, i = n // NPC, n % NPC
                    if i == 0:
                        idx = tr_plan.index(("x", s))
                        e.wait_ge(tr_moved, at(b, NTR, idx + 1))
                    if n >= 2:
                        e.wait_ge(pj_read, at(b, NPC * NT, n - 1))
                    w = wq1_s[:, :, i * NR:(i + 1) * NR] if i < NPC - 1 else wk1_s[:]
                    for k in range(KC):
                        last = MM(bank(n % 2), xnT[:, k, s * P:(s + 1) * P], w[:, k, :], start=(k == 0), stop=(k == KC - 1))
                    last.then_inc(pj_ready, 1)

                def values(s):
                    if s >= 1:
                        e.wait_ge(vp_moved, at(b, NT, s))
                    for gs in range(2):
                        for q in range(NQB):
                            for k in range(KC):
                                for g in range(4):
                                    c = (gs * NQB + q) * D1
                                    last = MM(psum[32 * g:32 * g + 32, 2, c:c + D1],
                                              xnT[:, k, s * P + q * QB:s * P + (q + 1) * QB],
                                              wv1_s[:, k, (4 * gs + g) * D1:(4 * gs + g + 1) * D1],
                                              start=(k == 0), stop=(k == KC - 1), tile_position=(0, 32 * g))
                    last.then_inc(vp_ready, 1)

                def scores(s):
                    e.wait_ge(tr_moved, at(b, NTR, tr_plan.index(("q", NPC * s + NPC - 1)) + 1))
                    for u in range(4):
                        gs, a2 = u // 2, u % 2
                        n = 4 * s + u
                        if n >= 2:
                            e.wait_ge(sT_done, at(b, 4 * NT, n - 1))
                        first = 1 if (s == 0 and a2 == 0) else 0
                        MM(bank(4 + n % 2), id16[:], mask16[:, first, :], start=True, stop=False, skip_group_check=True)
                        todo = [(a, part) for a in range(2) for part in range(2)
                                if not (first and a == 0 and part == 1)]
                        for a, part in todo:
                            q = 2 * a2 + a
                            kb = NQB * s + q - part
                            for g in range(4):
                                gp, ev = (4 * gs + g) // 2, g % 2
                                o = psum[32 * g:32 * g + 32, 4 + n % 2, :].rearrange(
                                    "p (a h c q) -> p a h c q", a=2, h=G1, c=2)[:, a, :, part, :]
                                last = MM(o, Kz[:, gp, ev, kb // NQB % KR, (kb % NQB) * QB:(kb % NQB + 1) * QB],
                                          QT1[:, 4 * gp:4 * gp + 4, q * QB:(q + 1) * QB],
                                          start=False, stop=True, tile_position=(0, 32 * g), skip_group_check=True)
                        last.then_inc(sc_ready, 1)

                def outputs(s):
                    for gp in range(GP1):
                        n = GP1 * s + gp
                        if n >= 1:
                            e.wait_ge(pv1_moved, at(b, 4 * NT, n))
                        if gp % 2 == 0:
                            e.wait_ge(pT_done, at(b, 4 * NT, 4 * s + gp + 2))
                        for q in range(NQB):
                            parts = [0] if (s == 0 and q == 0) else [0, 1]
                            for part in parts:
                                kb = NQB * s + q - part
                                pr = PT[:, gp // 2, q, :].rearrange("p (h c q) -> p h c q", h=G1, c=2)[:, :, part, :]
                                o = bank(6).rearrange("p (h s) -> p h s", h=G1)[:, :, q * QB:(q + 1) * QB]
                                last = MM(o, Vb[:, kb // NQB % VR, kb % NQB, gp, :], pr,
                                          start=(part == 0), stop=(part == parts[-1]))
                        last.then_inc(pv1_ready, 1)

                def out_project(s):
                    e.wait_ge(pv1_moved, at(b, 4 * NT, 4 * (s + 1)))
                    if s >= 1:
                        e.wait_ge(x_res, at(b, XR, 16 + s))
                    for c in range(16):
                        last = MM(bank(7)[:, 0:DM], OT1[:, c // 4, c % 4, :], wo1_s[:, c, :],
                                  start=(c == 0), stop=(c == 15))
                    last.then_inc(wo_ready, 1)

                turn(0, "x", 0)
                for s in range(NT + 2):
                    for i in range(NPC):
                        n = NPC * s + i
                        if n < NPC * NT:
                            project(n)
                        for g in steps[s][i]:
                            turn(*g)
                        if i == 1:
                            if s < NT:
                                values(s)
                            if 1 <= s <= NT:
                                scores(s - 1)
                            if s >= 2:
                                outputs(s - 2)
                        if i == NPC - 1 and s >= 2:
                            out_project(s - 2)
                leave(e, "pe")
                enter(e, "pe", b, 4)
                ffn_pe(e, b, 1)
                end_row(e, "pe")

        @block.scalar
        def _(e):
            with e.Fori(0, B) as b:
                enter(e, "act", b, 0)
                for t in range(NT + 3):
                    if t < NT:
                        e.wait_ge(xn_moved, at(b, 32, t + 1))
                        act.copy(xnT[:, :, t * P:(t + 1) * P],
                                 bank(t % 2)[:, 0:2 * P].rearrange("p (k s) -> p k s", k=KC)).then_inc(xT_ready, 1)
                    u = t - 1
                    if 0 <= u < NT:
                        e.wait_ge(qkv_ready, at(b, NT, u + 1))
                        if u >= 2:
                            e.wait_ge(lo_done, at(b, NT, u - 1))
                        ps = bank(2 + u % 2)
                        act.copy(qk32[:, u % 2, :, 8:16],
                                 ps[:, 0:HD0 * D0].rearrange("p (h d) -> p h d", d=D0)[:, :, 8:16])
                        act.copy(V0[:, u, :, 0:D0],
                                 ps[:, HD0 * D0:QKV0].rearrange("p (h d) -> p h d", d=D0)).then_inc(v0_out, 1)
                    u = t - 2
                    if 0 <= u < NT:
                        e.wait_ge(rope_done, at(b, NT, u + 1))
                        e.wait_ge(v0_out, at(b, NT, u + 1))
                        if u >= 2:
                            e.wait_ge(hT_ready, at(b, 3 * NT, 3 * (u - 1)))
                        if u == 0:
                            e.wait_ge(prep, at(b, 6, 6))
                        q16 = T16[:, u % 2, 0:H0, 0:64].rearrange("p h (r d) -> p h r d", r=4)
                        k16 = T16[:, u % 2, H0:HD0, 0:64].rearrange("p h (r d) -> p h r d", r=4)
                        act.copy(q16[:, :, 0:4:2, :], qk32[:, u % 2, 0:H0, :].unsqueeze(2).to_broadcast([P, H0, 2, D0]))
                        act.copy(k16[:, :, 0:2, :], qk32[:, u % 2, H0:HD0, :].unsqueeze(2).to_broadcast([P, KV0, 2, D0])
                                 ).then_inc(hi_done, 1)
                    u = t - 3
                    if 0 <= u < NT:
                        e.wait_ge(hT_ready, at(b, 3 * NT, 3 * u + 2))
                        act.copy(QT[0:65, 8:16, u * P:(u + 1) * P],
                                 bank16(5)[0:65, :].rearrange("p (h s) -> p h s", h=8)).then_inc(hT_act, 1)
                leave(e, "act")
                enter(e, "act", b, 1)

                def row(j):
                    pair = 2 * (slot_of("row", j) % 2)
                    e.wait_ge(mrow_ready, at(b, NHG, j + 1))
                    src = psum[64:65, pair:pair + 2, :].rearrange("p a n -> p (a n)").bitcast(F16)
                    act.copy(QT[64:65, 4 * (j // 2):4 * (j // 2) + 4, (j % 2) * HALF:(j % 2 + 1) * HALF],
                             src.rearrange("p (h s) -> p h s", h=4)).then_inc(mrow_moved, 1)

                row(0)
                for j in range(NHG):
                    for i in range(NK * G0):
                        n = j * NK * G0 + i
                        e.wait_ge(st_ready, at(b, 4 * NHG * NK, n + 1))
                        if n >= PR:
                            e.wait_ge(pv_done, at(b, NHG * NK, (n - PR) // G0 + 1))
                        act.activation(prob0[:, n % PR, :], bank(4 + n % 3), ACT.Exp, scale=float(D0) ** -0.5
                                       ).then_inc(exp_done, 1)
                    if j + 1 < NHG:
                        row(j + 1)
                    e.wait_ge(pv_done, at(b, NHG * NK, (j + 1) * NK))
                    if j >= 1:
                        e.wait_ge(oTr_ready, at(b, NHG, j))
                    act.copy(osum, bank(7)).then_inc(osum_done, 1)
                leave(e, "act")
                enter(e, "act", b, 2)
                for t in range(NT):
                    e.wait_ge(ot_ready, at(b, NT, t + 1))
                    if t >= 2:
                        e.wait_ge(wo_ready, at(b, 2 * NT, t - 1))
                    act.copy(oT[:, t % 2, :], bank(t % 2)[:, 0:DM]).then_inc(ot_moved, 1)
                ffn_act(e, b, 0)
                leave(e, "act")
                enter(e, "act", b, 3)

                def move(idx, kind, n):
                    if kind == "x":
                        e.wait_ge(xn_moved, at(b, 32, 16 + n + 1))
                        act.copy(xnT[:, :, n * P:(n + 1) * P],
                                 bank(3)[:, 0:2 * P].rearrange("p (k s) -> p k s", k=KC)).then_inc(tr_moved, 1)
                        return
                    e.wait_ge(tr_ready, at(b, NPC * NT, n + 1))
                    s, i = n // NPC, n % NPC
                    src = bank(3).rearrange("p (c s) -> p c s", c=4)
                    if i < NPC - 1:
                        if s >= 1:
                            e.wait_ge(sc_ready, at(b, 4 * NT, 4 * s))
                        act.copy(QT1[:, 4 * i:4 * i + 4, :], src).then_inc(tr_moved, 1)
                    else:
                        if s == 0:
                            e.wait_ge(prep4, at(b, 3, 3))
                        if s >= 2:
                            e.wait_ge(sc_ready, at(b, 4 * NT, 4 * (s - 1)))
                        act.copy(Kz[0:64, :, 0, s % KR, :], src[0:64, :, :])
                        act.copy(Kz[64:P, :, 1, s % KR, :], src[64:P, :, :]).then_inc(tr_moved, 1)

                def exps(s, u):
                    n = 4 * s + u
                    e.wait_ge(sub_done, at(b, 4 * NT, n + 1))
                    act.activation(sE[:, n % 2, :], sE[:, n % 2, :], ACT.Exp, scale=float(D1) ** -0.5).then_inc(ex_done, 1)

                move(0, "x", 0)
                for s in range(NT + 2):
                    for i in range(NPC):
                        for g in steps[s][i]:
                            move(*g)
                        if i == 1:
                            if s < NT:
                                e.wait_ge(vp_ready, at(b, NT, s + 1))
                                if s == 0:
                                    e.wait_ge(prep4, at(b, 3, 3))
                                if s >= VR:
                                    e.wait_ge(pv1_ready, at(b, 4 * NT, 4 * (s - 2)))
                                for g in range(4):
                                    src = psum[32 * g:32 * g + 32, 2, :].rearrange("p (a q d) -> p q a d", a=2, q=NQB)
                                    dst = Vb[32 * g:32 * g + 32, s % VR, :, g // 2::2, (g % 2) * D1:(g % 2 + 1) * D1]
                                    last = act.copy(dst, src)
                                last.then_inc(vp_moved, 1)
                            for gp in range(GP1 if s >= 2 else 0):
                                e.wait_ge(pv1_ready, at(b, 4 * NT, 4 * (s - 2) + gp + 1))
                                if s >= 3:
                                    e.wait_ge(wo_ready, at(b, 2 * NT, NT + s - 2))
                                act.copy(OT1[:, gp, :, :], bank(6).rearrange("p (h s) -> p h s", h=G1)).then_inc(pv1_moved, 1)
                                if gp == 1 and s <= NT:
                                    exps(s - 1, 0)
                                    exps(s - 1, 1)
                            if s == 1:
                                exps(0, 0)
                                exps(0, 1)
                        if i == 3 and 1 <= s <= NT:
                            exps(s - 1, 2)
                            exps(s - 1, 3)
                leave(e, "act")
                enter(e, "act", b, 4)
                ffn_act(e, b, 1)
                end_row(e, "act")

        @block.vector
        def _(e):
            e.wait_ge(loaded, 16 * NLOAD)
            dve.memset(wabs[:], 0.0).then_inc(dconst, 1)
            e.wait_ge(dconst, 1)
            raws = [(raw1, t1, P, KC), (raw2, t2, P, KC), (raw3, t3, None, len(FC0)), (raw4, u1, P, KC), (raw5, u2, P, len(FC1))]
            cnt = [DM * F0] * 3 + [DM * F1] * 2
            dve.tensor_reduce(wabs[:, 0:1], raw1, AX.XY, ALU.add, apply_absolute_value=True).then_inc(absdone, 1)
            dve.tensor_reduce(wabs[:, 1:2], raw2, AX.XY, ALU.add, apply_absolute_value=True).then_inc(absdone, 1)
            dve.tensor_reduce(wabs[:, 5:6], raw3[:, 0:5, :], AX.XY, ALU.add, apply_absolute_value=True).then_inc(dconst, 1)
            dve.tensor_reduce(wabs[0:64, 6:7], raw3[0:64, 5, :], AX.X, ALU.add, apply_absolute_value=True).then_inc(dconst, 1)
            e.wait_ge(dconst, 3)
            dve.tensor_tensor(wabs[:, 2:3], wabs[:, 5:6], wabs[:, 6:7], ALU.add).then_inc(absdone, 1)
            dve.tensor_reduce(wabs[:, 3:4], raw4, AX.XY, ALU.add, apply_absolute_value=True).then_inc(absdone, 1)
            dve.tensor_reduce(wabs[:, 4:5], raw5, AX.XY, ALU.add, apply_absolute_value=True).then_inc(absdone, 1)
            e.wait_ge(absall, 1)
            dve.tensor_scalar(thr[:, 2, 0:3], bank(0)[:, 0:3], 1.0 / cnt[0], 1e-8, ALU.mult, ALU.add).then_inc(thrdone, 1)
            dve.tensor_scalar(thr[:, 0, 3:5], bank(0)[:, 3:5], 1.0 / cnt[3], 0.7, ALU.mult, ALU.mult).then_inc(thrdone, 1)
            e.wait_ge(thrdone, 2)
            dve.tensor_scalar(thr[:, 0, 0:3], thr[:, 2, 0:3], 0.5, None, ALU.mult).then_inc(thrdone, 1)
            e.wait_ge(thrdone, 3)
            dve.tensor_scalar(thr[:, 1, :], thr[:, 0, :], -1.0, None, ALU.mult).then_inc(thrdone, 1)
            e.wait_ge(thrdone, 4)
            for i, (raw, q, p, kk) in enumerate(raws):
                lt, gt = (ALU.is_lt, ALU.is_gt) if i < 3 else (ALU.is_le, ALU.is_ge)
                cuts = [(P, slice(0, kk))] if i != 2 else [(P, slice(0, 5)), (64, slice(5, 6))]
                for j, (rows, ks) in enumerate(cuts):
                    m = (ks.stop - ks.start) * raw.shape[2]
                    r = raw[0:rows, ks, :].rearrange("p k f -> p (k f)")
                    o = q[0:rows, ks, :].rearrange("p k f -> p (k f)")
                    done = i + (1 if i > 2 else 0) + j
                    if done:
                        e.wait_ge(qstep, done)
                    dve.tensor_scalar(neg16[0:rows, 0:m], r, thr[0:rows, 1, i:i + 1], None, lt).then_inc(negdone, 1)
                    e.wait_ge(negdone, done + 1)
                    dve.scalar_tensor_tensor(o, r, thr[0:rows, 0, i:i + 1], neg16[0:rows, 0:m], gt, ALU.subtract).then_inc(qstep, 1)
            e.wait_ge(qstep, 6)
            e.drain().then_inc(quant, 5)
            with e.Fori(0, B) as b:
                enter(e, "dve", b, 0)
                e.wait_ge(x_loaded, at(b, 16, 16))
                for t in range(NT + 1):
                    if t < NT:
                        ln_stats(e, b, 0, t, None)
                    if t >= 1:
                        ln_norm(e, b, 0, t - 1)
                for t in range(NT + 3):
                    u = t - 1
                    if 0 <= u < NT:
                        e.wait_ge(v0_out, at(b, NT, u + 1))
                        if u >= 2:
                            e.wait_ge(hi_done, at(b, NT, u - 1))
                        if u >= 1:
                            e.wait_ge(rope_done, at(b, NT, u))
                        qk = bank(2 + u % 2)[:, 0:HD0 * D0].rearrange("p (h d) -> p h d", d=D0)[:, :, 0:8]
                        pair = qk.rearrange("p h (i two) -> p h i two", two=2)
                        rb = ropeB.rearrange("p h (i two) -> p h i two", two=2)
                        sn = s0[:, u, :].rearrange("p (i two) -> p i two", two=2)
                        dve.tensor_tensor(ropeA, qk, c0[:, u, :].unsqueeze(1).to_broadcast([P, HD0, 8]), ALU.mult)
                        for o in range(2):
                            last = dve.tensor_tensor(rb[:, :, :, o], pair[:, :, :, 1 - o],
                                                     sn[:, :, o].unsqueeze(1).to_broadcast([P, HD0, 4]), ALU.mult)
                        last.then_inc(rope_mul, 1)
                        e.wait_ge(rope_mul, at(b, NT, u + 1))
                        dve.tensor_tensor(qk32[:, u % 2, :, 0:8], ropeA, ropeB, ALU.add).then_inc(rope_done, 1)
                    u = t - 2
                    if 0 <= u < NT:
                        e.wait_ge(hi_done, at(b, NT, u + 1))
                        q16 = T16[:, u % 2, 0:H0, 0:64].rearrange("p h (r d) -> p h r d", r=4)
                        k16 = T16[:, u % 2, H0:HD0, 0:64].rearrange("p h (r d) -> p h r d", r=4)
                        dve.tensor_tensor(q16[:, :, 1:4:2, :], qk32[:, u % 2, 0:H0, :].unsqueeze(2).to_broadcast([P, H0, 2, D0]),
                                          q16[:, :, 0:4:2, :], ALU.subtract)
                        dve.tensor_tensor(k16[:, :, 2:4, :], qk32[:, u % 2, H0:HD0, :].unsqueeze(2).to_broadcast([P, KV0, 2, D0]),
                                          k16[:, :, 0:2, :], ALU.subtract).then_inc(lo_done, 1)
                    u = t - 3
                    if 0 <= u < NT:
                        if u == 0:
                            e.wait_ge(prep, at(b, 6, 6))
                        e.wait_ge(hT_ready, at(b, 3 * NT, 3 * u + 1))
                        dve.tensor_copy(QT[0:65, 0:8, u * P:(u + 1) * P],
                                        bank16(4)[0:65, :].rearrange("p (h s) -> p h s", h=8)).then_inc(hT_dve, 1)
                        e.wait_ge(hT_ready, at(b, 3 * NT, 3 * u + 3))
                        dve.tensor_copy(KT[0:65, :, u * P:(u + 1) * P],
                                        bank16(6)[0:65, 0:4 * P].rearrange("p (h s) -> p h s", h=4)).then_inc(hT_dve, 1)
                leave(e, "dve")
                enter(e, "dve", b, 1)
                for n, kind in enumerate(slots):
                    pair = 2 * (n % 2)
                    if kind == "max":
                        m = nth[n] - 1
                        j = m // 16
                        e.wait_ge(max_ready, at(b, 16 * NHG, m + 1))
                        if m % 16 == 0 and j >= 2:
                            e.wait_ge(mrow_ready, at(b, NHG, j - 1))
                        with nc.allow_low_precision(reason="a stabiliser: the same rounded value is in numerator and denominator"):
                            dve.tensor_reduce(mneg[:, j % 2, m % 16:m % 16 + 1], psum[:, pair:pair + 2, :], AX.XY, ALU.max,
                                              negate=True).then_inc(max_done, 1)
                    elif kind == "out":
                        j = nth[n] - 1
                        e.wait_ge(oTr_ready, at(b, NHG, j + 1))
                        o = bank(pair).rearrange("p (m d) -> p m d", d=32)
                        if j >= 1:
                            e.wait_ge(o_done, at(b, NHG, j))
                        dve.reciprocal(orec, o[:, :, D0]).then_inc(orec_done, 1)
                        e.wait_ge(orec_done, at(b, NHG, j + 1))
                        dst = otok[:, 4 * (j % 2):4 * (j % 2) + 4, (j // 2) * 64:(j // 2 + 1) * 64].rearrange(
                            "p t (h d) -> p t h d", d=D0)
                        dve.tensor_tensor(dst, o[:, :, 0:D0].rearrange("p (t h) d -> p t h d", h=4),
                                          orec.rearrange("p (t h) -> p t h", h=4).unsqueeze(3).to_broadcast([P, 4, 4, D0]),
                                          ALU.mult).then_inc(o_done, 1)
                leave(e, "dve")
                enter(e, "dve", b, 2)
                for t in range(NT + 1):
                    if t < NT:
                        e.wait_ge(wo_ready, at(b, 2 * NT, t + 1))
                        dve.tensor_tensor(x[:, t, :], bank(2 + t % 2)[:, 0:DM], x[:, t, :], ALU.add).then_inc(x_res, 1)
                        ln_stats(e, b, 1, t, t + 1)
                    if t >= 1:
                        ln_norm(e, b, 1, t - 1)
                ffn_dve(e, b, 0)
                leave(e, "dve")
                enter(e, "dve", b, 3)

                def rope(n):
                    s = n // NPC
                    e.wait_ge(pj_ready, at(b, NPC * NT, n + 1))
                    if n >= 2:
                        e.wait_ge(pj_rot, at(b, NPC * NT, n - 1))
                    ps = bank(n % 2)
                    dve.tensor_tensor(rA[:, n % 2, :].rearrange("p (h c) -> p h c", c=32), ps.rearrange("p (h c) -> p h c", c=32),
                                      c1[:, s, :].unsqueeze(1).to_broadcast([P, 16, 32]), ALU.mult)
                    half = ps.rearrange("p (h a c) -> p h a c", a=2, c=32)
                    rb = rB[:, n % 2, :].rearrange("p (h a c) -> p h a c", a=2, c=32)
                    for a in range(2):
                        last = dve.tensor_tensor(rb[:, :, a, :], half[:, :, 1 - a, :],
                                                 s1[:, s, a, :].unsqueeze(1).to_broadcast([P, 8, 32]), ALU.mult)
                    last.then_inc(pj_read, 1)

                def turn_max(s, u):
                    n = 4 * s + u
                    e.wait_ge(sc_ready, at(b, 4 * NT, n + 1))
                    if n >= 2:
                        e.wait_ge(sub_done, at(b, 4 * NT, n - 1))
                    dve.transpose(sT[:, n % 2, :], bank(4 + n % 2)).then_inc(sT_done, 1)
                    e.wait_ge(sT_done, at(b, 4 * NT, n + 1))
                    dve.tensor_reduce(smax[:, n % 2, :], sT[:, n % 2, :].rearrange("p (m c) -> p m c", c=64), AX.X, ALU.max
                                      ).then_inc(mx_done, 1)

                def sums(s, u):
                    n = 4 * s + u
                    e.wait_ge(ex_done, at(b, 4 * NT, n + 1))
                    if n >= 2:
                        e.wait_ge(nrm_done, at(b, 4 * NT, n - 1))
                    dve.tensor_reduce(ssum[:, n % 2, :], sE[:, n % 2, :].rearrange("p (m c) -> p m c", c=64), AX.X, ALU.add
                                      ).then_inc(sm_done, 1)
                    e.wait_ge(sm_done, at(b, 4 * NT, n + 1))
                    dve.reciprocal(ssum[:, n % 2, :], ssum[:, n % 2, :]).then_inc(rc_done, 1)

                def turn_back(s, u):
                    n = 4 * s + u
                    e.wait_ge(nrm_done, at(b, 4 * NT, n + 1))
                    if u == 0 and s >= 1:
                        e.wait_ge(pv1_ready, at(b, 4 * NT, 4 * s))
                    gs, a2 = u // 2, u % 2
                    dve.transpose(PT[:, gs, 2 * a2:2 * a2 + 2, :].rearrange("p q n -> p (q n)"), sE[:, n % 2, :]).then_inc(pT_done, 1)

                for s in range(NT + 2):
                    live = 1 <= s <= NT
                    for i in range(NPC):
                        if s < NT:
                            rope(NPC * s + i)
                        if i == 1 and live:
                            turn_max(s - 1, 0)
                            turn_max(s - 1, 1)
                        if i == 2 and live:
                            sums(s - 1, 0)
                            sums(s - 1, 1)
                            turn_max(s - 1, 2)
                        if i == 3 and live:
                            turn_max(s - 1, 3)
                            turn_back(s - 1, 0)
                            sums(s - 1, 2)
                            turn_back(s - 1, 1)
                        if i == 4 and live:
                            sums(s - 1, 3)
                            turn_back(s - 1, 2)
                            turn_back(s - 1, 3)
                    if s >= 2:
                        t = s - 2
                        e.wait_ge(wo_ready, at(b, 2 * NT, NT + t + 1))
                        dve.tensor_tensor(x[:, t, :], bank(7)[:, 0:DM], x[:, t, :], ALU.add).then_inc(x_res, 1)
                        ln_stats(e, b, 3, t, 16 + t + 1)
                        if t >= 1:
                            ln_norm(e, b, 3, t - 1)
                ln_norm(e, b, 3, NT - 1)
                leave(e, "dve")
                enter(e, "dve", b, 4)
                ffn_dve(e, b, 1)
                end_row(e, "dve")

        @block.gpsimd
        def _(e):
            pool.memset(ones[:], 1.0).then_inc(consts, 1)
            pool.memset(mhalf[:], -0.5).then_inc(consts, 1)
            e.wait_ge(loaded, 16 * NLOAD)
            pool.tensor_copy(id16[:], id32[:]).then_inc(consts, 1)
            e.drain().then_inc(consts, 1)
            with e.Fori(0, B) as b:
                enter(e, "pool", b, 0)
                e.wait_ge(quant, 5)
                for i, (dst, value) in enumerate((
                        (T16[:, :, 0:H0, 64:65], 0.0), (T16[:, :, H0:HD0, 64:65], 1.0),
                        (V0[:, :, :, D0 + 1:32], 0.0), (V0[:, :, :, D0:D0 + 1], 1.0),
                        (QT[64:P, :, :].bitcast(mybir.dt.uint32), 0), (KT[64:P, :, :].bitcast(mybir.dt.uint32), 0))):
                    if i:
                        e.wait_ge(prep, i)
                    pool.memset(dst, value).then_inc(prep, 1)
                e.wait_ge(prep, at(b, 6, 6))
                for t in range(NT):
                    ln_pow(e, b, 0, t)
                leave(e, "pool")
                enter(e, "pool", b, 1)
                leave(e, "pool")
                enter(e, "pool", b, 2)
                for t in range(NT):
                    ln_pow(e, b, 1, t)
                ffn_pool(e, b, 0)
                for t in range(NT):
                    ln_pow(e, b, 2, t)
                leave(e, "pool")
                enter(e, "pool", b, 3)
                for i, dst in enumerate((Kz[0:64, :, 1, :, :], Kz[64:P, :, 0, :, :], Vb)):
                    if i:
                        e.wait_ge(prep4, i)
                    pool.memset(dst, 0.0).then_inc(prep4, 1)

                def rotate(n):
                    e.wait_ge(pj_read, at(b, NPC * NT, n + 1))
                    if n >= 2:
                        e.wait_ge(tr_ready, at(b, NPC * NT, n - 1))
                    pool.tensor_tensor(rot[:, n % 2, :], rA[:, n % 2, :], rB[:, n % 2, :], ALU.add).then_inc(pj_rot, 1)

                def minus_max(s, u):
                    n = 4 * s + u
                    e.wait_ge(mx_done, at(b, 4 * NT, n + 1))
                    if n >= 2:
                        e.wait_ge(pT_done, at(b, 4 * NT, n - 1))
                    pool.tensor_tensor(sE[:, n % 2, :].rearrange("p (m c) -> p m c", c=64),
                                       sT[:, n % 2, :].rearrange("p (m c) -> p m c", c=64),
                                       smax[:, n % 2, :].unsqueeze(2).to_broadcast([P, 8, 64]), ALU.subtract).then_inc(sub_done, 1)

                def normalise(s, u):
                    n = 4 * s + u
                    e.wait_ge(rc_done, at(b, 4 * NT, n + 1))
                    v = sE[:, n % 2, :].rearrange("p (m c) -> p m c", c=64)
                    pool.tensor_tensor(v, v, ssum[:, n % 2, :].unsqueeze(2).to_broadcast([P, 8, 64]), ALU.mult).then_inc(nrm_done, 1)

                for s in range(NT + 2):
                    live = 1 <= s <= NT
                    for i in range(NPC):
                        if s < NT:
                            rotate(NPC * s + i)
                        if live and i == 1:
                            minus_max(s - 1, 0)
                            minus_max(s - 1, 1)
                        if live and i == 2:
                            normalise(s - 1, 0)
                            normalise(s - 1, 1)
                        if live and i == 3:
                            minus_max(s - 1, 2)
                            minus_max(s - 1, 3)
                        if live and i == 4:
                            normalise(s - 1, 2)
                            normalise(s - 1, 3)
                    if s >= 2:
                        ln_pow(e, b, 3, s - 2)
                leave(e, "pool")
                enter(e, "pool", b, 4)
                ffn_pool(e, b, 1)
                e.wait_ge(row_end, 4)
                pool.sem_clear(row_sems)
                for other in cleared:
                    e.drain().then_inc(cleared[other], 1)


def tables():
    pos = np.arange(S, dtype=np.float32)
    inv0 = (1.0 / 10000.0 ** (np.arange(0, D0 // 2, 2, dtype=np.float32) / np.float32(D0 // 2))).astype(np.float32)
    a0 = pos[:, None] * inv0[None, :]
    cos0 = np.repeat(np.cos(a0), 2, axis=1).astype(np.float32)
    sin0 = np.stack([-np.sin(a0), np.sin(a0)], axis=-1).reshape(S, 8).astype(np.float32)
    inv1 = (1.0 / 10000.0 ** (np.arange(0, D1, 2, dtype=np.float32) / np.float32(D1))).astype(np.float32)
    a1 = pos[:, None] * inv1[None, :]
    cos1 = np.cos(a1).astype(np.float32)
    sin1 = np.concatenate([-np.sin(a1), np.sin(a1)], axis=1).astype(np.float32)
    key, query = np.arange(QB)[:, None], np.arange(QB)[None, :]
    own = np.where(key <= query, 0.0, MASKED)
    before = np.where(key >= query, 0.0, MASKED)
    block = np.stack([own, before], axis=1)
    mask = np.zeros((4, QB, 2, 2, G1, 2, QB), np.float16)
    mask[:] = block[None, :, None, None, None, :, :]
    mask[:, :, 1, 0, :, 1, :] = MASKED
    return cos0, sin0, cos1, sin1, np.eye(P, dtype=np.float32), mask.reshape(P, 2 * HALF)


def kernel(**inputs):
    import concourse.bacc as bacc
    from concourse.bass_utils import run_bass_kernel_spmd

    a = {k: np.ascontiguousarray(v) for k, v in inputs.items()}
    cos0, sin0, cos1, sin1, ident, mask = tables()
    wq1 = a["L1_attn_wq"].T.reshape(DM, GP1, 2, G1, D1).transpose(0, 1, 3, 2, 4).reshape(DM, H1 * D1)
    wo1 = a["L1_attn_wo"].T.reshape(GP1, 2, G1, D1, DM).transpose(0, 2, 1, 3, 4).reshape(H1 * D1, DM)
    arrays = {
        "x_in": a["L0_attn_hidden_states"],
        "cos0": cos0, "sin0": sin0, "cos1": cos1, "sin1": sin1, "ident": ident, "mask": mask,
        "wqkv0": np.concatenate([a["L0_attn_Wq"], a["L0_attn_Wk"], a["L0_attn_Wv"]], axis=1),
        "wo0": a["L0_attn_Wo"],
        "w1": a["L0_ffn_w1"].T, "w2": a["L0_ffn_w2"].T, "w3": a["L0_ffn_w3"].T,
        "wq1": wq1, "wk1": a["L1_attn_wk"].T, "wv1": a["L1_attn_wv"].T, "wo1": wo1,
        "f1w1": a["L1_ffn_w1"].T, "f1b1": a["L1_ffn_b1"].reshape(len(FC1), P).T, "f1w2": a["L1_ffn_w2"].T, "f1b2": a["L1_ffn_b2"],
    }
    arrays = {k: np.ascontiguousarray(v) for k, v in arrays.items()}
    nc = bacc.Bacc("TRN2", target_bir_lowering=False, num_devices=1)
    args = [nc.dram_tensor(k, v.shape, mybir.dt.from_np(v.dtype), kind="ExternalInput").ap() for k, v in arrays.items()]
    out = nc.dram_tensor("out_0", (B, S, DM), F32, kind="ExternalOutput").ap()
    build(nc, *args, out)
    r = run_bass_kernel_spmd(nc, [arrays], core_ids=[0])
    return r.results[0]["out_0"]
```

```python
from contextlib import ExitStack

import numpy as np

import concourse.bass as bass
from concourse import mybir

F32 = mybir.dt.float32
F16 = mybir.dt.float16
ALU = mybir.AluOpType
ACT = mybir.ActivationFunctionType
AX = mybir.AxisListType

P = 128
B, S, DM = 2, 1024, 256
NT = S // P
KC = DM // P
EPS = 1e-5
H0, KV0, D0 = 16, 4, 16
G0 = H0 // KV0
HD0 = H0 + KV0
QKV0 = (H0 + 2 * KV0) * D0
F0 = 704
FC0 = [P] * (F0 // P) + [F0 % P]
H1, KV1, D1, WIN = 32, 8, 64, 32
G1 = H1 // KV1
QB = 32
NQB = P // QB
GP1 = KV1 // 2
F1 = 1024
FC1 = [P] * (F1 // P)
MASKED = -60000.0
HALF = 512


def build(nc, x_in, cos0, sin0, cos1, sin1, ident, mask, wqkv0, wo0, w1, w2, w3,
          wq1, wk1, wv1, wo1, f1w1, f1b1, f1w2, f1b2, out):
    ctx = ExitStack()
    with ctx:
        def sb(name, shape, dt=F32):
            return ctx.enter_context(nc.sbuf_tensor(name, shape, dt))

        def sem(name):
            return ctx.enter_context(nc.semaphore(name))

        psum = ctx.enter_context(nc.psum_tensor("psum", [P, 8, HALF], F32))

        def bank(i):
            return psum[:, i, :]

        def bank16(i):
            return psum[:, i, :].bitcast(F16)

        id32 = sb("id32", [P, P])
        id16 = sb("id16", [P, P], F16)
        mask16 = sb("mask16", [P, 2, HALF], F16)
        c0 = sb("c0", [P, NT, 8])
        s0 = sb("s0", [P, NT, 8])
        c1 = sb("c1", [P, NT, 32])
        s1 = sb("s1", [P, NT, 2, 32])
        wqkv0_s = sb("wqkv0_s", [P, KC, QKV0])
        wo0_s = sb("wo0_s", [P, KC, DM])
        wq1_s = sb("wq1_s", [P, KC, H1 * D1])
        wk1_s = sb("wk1_s", [P, KC, KV1 * D1])
        wv1_s = sb("wv1_s", [P, KC, KV1 * D1])
        wo1_s = sb("wo1_s", [P, H1 * D1 // P, DM])
        t1 = sb("t1", [P, KC, F0], F16)
        t2 = sb("t2", [P, KC, F0], F16)
        t3 = sb("t3", [P, len(FC0), DM], F16)
        u1 = sb("u1", [P, KC, F1], F16)
        u2 = sb("u2", [P, len(FC1), DM], F16)
        b1c = sb("b1c", [P, len(FC1)])
        b2r = sb("b2r", [P, DM])
        wabs = sb("wabs", [P, 8])
        wtot = sb("wtot", [P, 8])
        thr = sb("thr", [P, 3, 5])
        x = sb("x", [P, NT, DM])
        stats = sb("stats", [P, NT, 6])
        mv = sb("mv", [P, NT, 2])
        rstd = sb("rstd", [P, NT])
        mhalf = sb("mhalf", [P, 1])
        xn = sb("xn", [P, NT, DM])
        xnT = sb("xnT", [P, KC, S])
        otok = sb("otok", [P, NT, DM])

        REGION = 106 * 1024 // 4
        region = sb("region", [P, REGION])
        cut = [0]

        def share(cols, dt=F32):
            words = cols if dt == F32 else cols // 2
            a = region[:, cut[0]:cut[0] + words]
            cut[0] += words
            assert cut[0] <= REGION, cut[0]
            return a if dt == F32 else a.bitcast(dt)

        cut[0] = 0
        QT = share(H0 * S, F16).rearrange("p (h s) -> p h s", h=H0)
        KT = share(KV0 * S, F16).rearrange("p (h s) -> p h s", h=KV0)
        V0 = share(NT * KV0 * 32).rearrange("p (t g d) -> p t g d", t=NT, g=KV0)
        PR = 8
        prob0 = share(PR * HALF).rearrange("p (r n) -> p r n", r=PR)
        osum = share(HALF)
        orec = share(NQB * G0)
        mneg = share(2 * G0 * NT, F16).rearrange("p (r n) -> p r n", r=2)
        p1_only = cut[0]
        qk32 = share(2 * HD0 * D0).rearrange("p (r h d) -> p r h d", r=2, h=HD0)
        ropeA = share(HD0 * 8).rearrange("p (h d) -> p h d", h=HD0)
        ropeB = share(HD0 * 8).rearrange("p (h d) -> p h d", h=HD0)
        TW = 66
        T16 = share(2 * HD0 * TW, F16).rearrange("p (r h d) -> p r h d", r=2, h=HD0)
        raw1 = share(KC * F0)
        raw2 = share(KC * F0)
        raw3 = share(len(FC0) * DM)
        raw4 = share(KC * F1)
        raw5 = share(len(FC1) * DM)
        QN = 2048
        below = region[:, p1_only:p1_only + QN // 2].bitcast(F16)
        cut[0] = 0
        xhi = share(KC * S, F16).rearrange("p (k s) -> p k s", k=KC)
        xlo = share(KC * S, F16).rearrange("p (k s) -> p k s", k=KC)
        NFR = 4
        gate = share(NFR * HALF).rearrange("p (r n) -> p r n", r=NFR)
        hid = share(NFR * HALF).rearrange("p (r n) -> p r n", r=NFR)
        hhi = share(16 * HALF, F16).rearrange("p (f n) -> p f n", f=16)
        hlo = share(16 * HALF, F16).rearrange("p (f n) -> p f n", f=16)
        oT = share(2 * DM).rearrange("p (r n) -> p r n", r=2)
        cut[0] = 0
        NR = KV1 * D1
        NPC = (H1 + KV1) * D1 // NR
        rA = share(2 * NR).rearrange("p (r n) -> p r n", r=2)
        rB = share(2 * NR).rearrange("p (r n) -> p r n", r=2)
        rot = share(2 * NR).rearrange("p (r n) -> p r n", r=2)
        QT1 = share(16 * P).rearrange("p (c s) -> p c s", c=16)
        KR = 3
        Kz = share(GP1 * 2 * KR * P).rearrange("p (g e r s) -> p g e r s", g=GP1, e=2, r=KR)
        VR = 4
        Vb = share(VR * NQB * GP1 * P).rearrange("p (b g d) -> p b g d", b=VR * NQB, g=GP1)
        sT = share(2 * HALF).rearrange("p (r n) -> p r n", r=2)
        sE = share(2 * HALF).rearrange("p (r n) -> p r n", r=2)
        NM = NQB * G1
        smax = share(2 * NM).rearrange("p (r n) -> p r n", r=2)
        ssum = share(2 * NM).rearrange("p (r n) -> p r n", r=2)
        mboth = share(2 * NM).rearrange("p (r n) -> p r n", r=2)
        sboth = share(2 * NM).rearrange("p (r n) -> p r n", r=2)
        PT = share(GP1 * HALF).rearrange("p (g n) -> p g n", g=GP1)
        OT1 = share(GP1 * G1 * P).rearrange("p (g h s) -> p g h s", g=GP1, h=G1)

        loaded = sem("loaded")
        raw_loaded = sem("raw_loaded")
        rest_loaded = sem("rest_loaded")
        consts = sem("consts")
        wzero = sem("wzero")
        absdone = sem("absdone")
        absall = sem("absall")
        thrdone = sem("thrdone")
        qstep = sem("qstep")
        quant = sem("quant")
        x_loaded = sem("x_loaded")
        x_stored = sem("x_stored")
        x_free = sem("x_free")
        cleared = {e: sem(f"cleared_{e}") for e in ("pe", "act", "dve", "sp")}
        row_end = sem("row_end")
        phase_end = {e: sem(f"phase_end_{e}") for e in ("pe", "act", "dve", "pool")}
        stat_done = sem("stat_done")
        var_ready = sem("var_ready")
        eps_added = sem("eps_added")
        rstd_ready = sem("rstd_ready")
        xn_ready = sem("xn_ready")
        xn_moved = sem("xn_moved")
        xT_ready = sem("xT_ready")
        x_res = sem("x_res")
        x_copied = sem("x_copied")
        qkv_ready = sem("qkv_ready")
        v0_out = sem("v0_out")
        rope_mul = sem("rope_mul")
        rope_done = sem("rope_done")
        hi_done = sem("hi_done")
        lo_done = sem("lo_done")
        hT_ready = sem("hT_ready")
        hT_dve = sem("hT_dve")
        hT_act = sem("hT_act")
        prep = sem("prep")
        prep4 = sem("prep4")
        max_ready = sem("max_ready")
        max_done = sem("max_done")
        mrow_ready = sem("mrow_ready")
        mrow_moved = sem("mrow_moved")
        st_ready = sem("st_ready")
        exp_done = sem("exp_done")
        pv_done = sem("pv_done")
        osum_done = sem("osum_done")
        oTr_ready = sem("oTr_ready")
        orec_done = sem("orec_done")
        o_done = sem("o_done")
        ot_ready = sem("ot_ready")
        ot_moved = sem("ot_moved")
        wo_ready = sem("wo_ready")
        hi2_done = sem("hi2_done")
        lo2_done = sem("lo2_done")
        up_ready = sem("up_ready")
        gate_done = sem("gate_done")
        hid_done = sem("hid_done")
        hhi_done = sem("hhi_done")
        hlo_done = sem("hlo_done")
        down_ready = sem("down_ready")
        b2_done = sem("b2_done")
        pj_ready = sem("pj_ready")
        pj_read = sem("pj_read")
        pj_rot = sem("pj_rot")
        tr_ready = sem("tr_ready")
        tr_moved = sem("tr_moved")
        vp_ready = sem("vp_ready")
        vp_moved = sem("vp_moved")
        sc_ready = sem("sc_ready")
        sT_done = sem("sT_done")
        mx_done = sem("mx_done")
        mb_done = sem("mb_done")
        sb_done = sem("sb_done")
        sub_done = sem("sub_done")
        ex_done = sem("ex_done")
        sm_done = sem("sm_done")
        rc_done = sem("rc_done")
        nrm_done = sem("nrm_done")
        pT_done = sem("pT_done")
        pv1_ready = sem("pv1_ready")
        pv1_moved = sem("pv1_moved")

        row_sems = range(row_end.num, pv1_moved.num + 1)

        def at(b, per, n):
            assert 0 <= n <= per, (n, per)
            return n

        PH = 5
        NLOAD, NRAW, NREST = 4, 6, 10
        names = ("pe", "act", "dve", "pool")

        def enter(e, me, b, ph):
            for other in names:
                if other != me and ph > 0:
                    e.wait_ge(phase_end[other], at(b, PH, ph))

        def end_row(e, me):
            e.drain().then_inc(row_end, 1)
            e.wait_ge(cleared[me], 1)
            e.sem_clear(cleared[me])

        def leave(e, me):
            e.drain().then_inc(phase_end[me], 1)

        block = ctx.enter_context(nc.Block())
        dve, act, pe, pool, sp = nc.vector, nc.scalar, nc.tensor, nc.gpsimd, nc.sync

        XR = 32

        def ln_stats(e, b, use, t, after_res):
            if after_res:
                e.wait_ge(x_res, at(b, XR, after_res))
            src = otok if use == 0 else x
            dve.bn_stats(stats[:, t, :], src[:, t, :]).then_inc(stat_done, 1)
            e.wait_ge(stat_done, at(b, 32, 8 * use + t + 1))
            dve.bn_aggr(mv[:, t, :], stats[:, t, :]).then_inc(var_ready, 1)

        def ln_norm(e, b, use, t):
            i = 8 * use + t
            e.wait_ge(rstd_ready, at(b, 32, i + 1))
            if i >= 8:
                e.wait_ge(xn_moved, at(b, 32, i - 7))
            src = otok if use == 0 else x
            dve.tensor_scalar(xn[:, t, :], src[:, t, :], mv[:, t, 0:1], rstd[:, t:t + 1],
                              ALU.subtract, ALU.mult).then_inc(xn_ready, 1)

        def ln_pow(e, b, use, t):
            i = 8 * use + t
            e.wait_ge(var_ready, at(b, 32, i + 1))
            pool.tensor_scalar(rstd[:, t:t + 1], mv[:, t, 1:2], EPS, None, ALU.add).then_inc(eps_added, 1)
            e.wait_ge(eps_added, at(b, 32, i + 1))
            pool.tensor_tensor(rstd[:, t:t + 1], rstd[:, t:t + 1], mhalf[:], ALU.pow).then_inc(rstd_ready, 1)

        def transpose_tile(e, b, use, t, dst, ready=None):
            i = 8 * use + t
            e.wait_ge(xn_ready, at(b, 32, i + 1))
            for k in range(KC):
                last = pe.transpose(dst[:, k, :], xn[:, t, k * P:(k + 1) * P], id32[:])
            last.then_inc(xn_moved, 1)

        def stat_kind(kind_list, n):
            return sum(1 for k in kind_list[:n + 1] if k == kind_list[n])

        NHG = 2 * KV0
        NK = S // P
        PER_KT = 2
        HEAD_START = 20
        OUT_KT = 2
        SUM_ACT = 5
        ROW_KT = 6
        ROW_ACT = 29
        slots, plan = ["max"] * 16 + ["row"] + ["max"] * (HEAD_START - 16), []
        first_slots = len(slots)
        for j in range(NHG):
            row = []
            for kt in range(NK):
                todo = []
                todo += ["max"] * min(PER_KT, 16 * NHG - slots.count("max"))
                if kt == OUT_KT and j >= 1:
                    todo += ["out"]
                if kt == ROW_KT and j + 1 < NHG:
                    todo += ["row"]
                row.append((len(slots), todo))
                slots += todo
            plan.append(row)
        slots.append("out")
        nth = [stat_kind(slots, n) for n in range(len(slots))]
        PV_LAG = 1

        def ffn_sizes(layer):
            return FC0 if layer == 0 else FC1

        def up_base(layer):
            return 0 if layer == 0 else 2 * len(FC0)

        NUP = 2 * len(FC0) + 2 * len(FC1)

        tr_plan = [("x", 0)]
        steps = []
        for s in range(NT + 2):
            st = []
            for i in range(NPC):
                n = NPC * s + i
                group = []
                if i == NPC - 1 and s + 1 < NT:
                    group.append((len(tr_plan), "x", s + 1))
                    tr_plan.append(("x", s + 1))
                if 2 <= n < NPC * NT + 2:
                    group.append((len(tr_plan), "q", n - 2))
                    tr_plan.append(("q", n - 2))
                st.append(group)
            steps.append(st)
        NTR = len(tr_plan)

        TURN_T = 6
        TURN_F = 2

        def turn_chunk(e, b, layer, c):
            if c == 1:
                e.wait_ge(lo2_done, at(b, 8, 4 * layer + 2))
            view = psum[:, 0:2, :]
            for i in range(4):
                transpose_tile(e, b, 1 + 2 * layer, 4 * c + i, view[:, :, i * P:(i + 1) * P])

        def high_chunk(e, b, layer, c):
            e.wait_ge(xn_moved, at(b, 32, (8 if layer == 0 else 24) + 4 * (c + 1)))
            for k in range(KC):
                act.copy(xhi[:, k, c * HALF:(c + 1) * HALF], bank(k)).then_inc(hi2_done, 1)

        def low_chunk(e, b, layer, c):
            for k in range(KC):
                e.wait_ge(hi2_done, at(b, 8, 4 * layer + 2 * c + k + 1))
                dve.tensor_tensor(xlo[:, k, c * HALF:(c + 1) * HALF], bank(k), xhi[:, k, c * HALF:(c + 1) * HALF],
                                  ALU.subtract).then_inc(lo2_done, 1)

        def ffn_pe(e, b, layer):
            MM = pe.matmul
            sizes = ffn_sizes(layer)
            nf = len(sizes)
            base = up_base(layer)

            def up(c):
                if c == 0:
                    e.wait_ge(lo2_done, at(b, 8, 4 * layer + 2))
                else:
                    e.wait_ge(lo2_done, at(b, 8, 4 * layer + 4))
                for f, size in enumerate(sizes):
                    n = c * nf + f
                    if layer == 0:
                        if n < 2:
                            e.wait_ge(x_res, at(b, XR, NT - 1 + n))
                        if n >= 2:
                            e.wait_ge(gate_done, at(b, NUP, base + n - 1))
                            e.wait_ge(hid_done, at(b, 12, n - 1))
                        outs = ((t1, bank(2 + n % 2)), (t2, bank(4 + n % 2)))
                    else:
                        if n >= 4:
                            e.wait_ge(gate_done, at(b, NUP, base + n - 3))
                        outs = ((u1, bank(2 + n % 4)),)
                    for w, o in outs:
                        for k in range(KC):
                            for part, xs in enumerate((xhi, xlo)):
                                last = MM(o[0:size, :], w[:, k, f * P:f * P + size], xs[:, k, c * HALF:(c + 1) * HALF],
                                          start=(k == 0 and part == 0), stop=(k == KC - 1 and part == 1))
                    last.then_inc(up_ready, 1)
                    if c == 0 and f == TURN_F:
                        turn_chunk(e, b, layer, 1)

            def down(c):
                w = t3 if layer == 0 else u2
                for i in range(4):
                    m = 4 * c + i
                    if m >= 2:
                        e.wait_ge(x_res, at(b, XR, (8 if layer == 0 else 24) + m - 1))
                    for f, size in enumerate(sizes):
                        if i == 0:
                            e.wait_ge(hlo_done, at(b, NUP, base + c * nf + f + 1))
                        for part, hs in enumerate((hhi, hlo)):
                            last = MM(bank(6 + m % 2)[:, 0:DM], hs[0:size, 8 * c + f, i * P:(i + 1) * P], w[0:size, f, :],
                                      start=(f == 0 and part == 0), stop=(f == nf - 1 and part == 1))
                    last.then_inc(down_ready, 1)

            up(0)
            up(1)
            down(0)
            down(1)

        def slot_of(kind, j):
            return [n for n in range(len(slots)) if slots[n] == kind][j]

        def ffn_act(e, b, layer):
            sizes = ffn_sizes(layer)
            nf = len(sizes)
            base = up_base(layer)
            for c in range(2):
                for f, size in enumerate(sizes):
                    n = c * nf + f
                    e.wait_ge(up_ready, at(b, NUP, base + n + 1))
                    if layer == 0:
                        if n >= NFR:
                            e.wait_ge(hid_done, at(b, 12, n - NFR + 1))
                        act.activation(gate[0:size, n % NFR, :], bank(2 + n % 2)[0:size, :], ACT.Sigmoid).then_inc(gate_done, 1)
                    else:
                        if n >= NFR:
                            e.wait_ge(hlo_done, at(b, NUP, base + n - NFR + 1))
                        act.activation(hid[0:size, n % NFR, :], bank(2 + n % 4)[0:size, :], ACT.Gelu,
                                       bias=b1c[:, f:f + 1]).then_inc(gate_done, 1)
                    if c == 0 and f == TURN_F:
                        high_chunk(e, b, layer, 1)

        def ffn_dve(e, b, layer):
            sizes = ffn_sizes(layer)
            nf = len(sizes)
            base = up_base(layer)

            def low(n):
                c, f = n // nf, n % nf
                size = sizes[f]
                e.wait_ge(hid_done if layer == 0 else gate_done,
                          at(b, 12 if layer == 0 else NUP, n + 1 if layer == 0 else base + n + 1))
                dve.tensor_copy(hhi[0:size, 8 * c + f, :], hid[0:size, n % NFR, :]).then_inc(hhi_done, 1)
                e.wait_ge(hhi_done, at(b, NUP, base + n + 1))
                dve.tensor_tensor(hlo[0:size, 8 * c + f, :], hid[0:size, n % NFR, :], hhi[0:size, 8 * c + f, :],
                                  ALU.subtract).then_inc(hlo_done, 1)

            for c in range(2):
                for f, size in enumerate(sizes):
                    n = c * nf + f
                    if layer == 0:
                        e.wait_ge(gate_done, at(b, NUP, base + n + 1))
                        if n >= NFR:
                            e.wait_ge(hlo_done, at(b, NUP, base + n - NFR + 1))
                        dve.tensor_tensor(hid[0:size, n % NFR, :], bank(4 + n % 2)[0:size, :], gate[0:size, n % NFR, :],
                                          ALU.mult).then_inc(hid_done, 1)
                    if n >= 1:
                        low(n - 1)
                    if c == 0 and f == TURN_F:
                        low_chunk(e, b, layer, 1)
            low(2 * nf - 1)
            for t in range(NT):
                done = (8 if layer == 0 else 24) + t
                e.wait_ge(down_ready, at(b, 2 * NT, NT * layer + t + 1))
                if layer == 1:
                    e.wait_ge(b2_done, at(b, NT, t + 1))
                dve.tensor_tensor(x[:, t, :], bank(6 + t % 2)[:, 0:DM], x[:, t, :], ALU.add).then_inc(x_res, 1)
                if layer == 0:
                    ln_stats(e, b, 2, t, done + 1)
                    if t >= 1:
                        ln_norm(e, b, 2, t - 1)
            if layer == 0:
                ln_norm(e, b, 2, NT - 1)

        def ffn_pool(e, b, layer):
            if layer == 1:
                for t in range(NT):
                    e.wait_ge(xn_ready, at(b, 32, 24 + t + 1))
                    pool.tensor_tensor(x[:, t, :], x[:, t, :], b2r[:], ALU.add).then_inc(b2_done, 1)
        @block.sync
        def _(e):
            def load_x(b):
                for half in range(2):
                    e.dma_start(otok[:, 4 * half:4 * half + 4, :],
                                x_in[b, half * HALF:(half + 1) * HALF, :].rearrange("(t p) d -> p t d", p=P)
                                ).then_inc(x_loaded, 16)

            load_x(0)
            for dst, src in (
                    (id32[:], ident),
                    (wqkv0_s[:], wqkv0.rearrange("(k p) f -> p k f", p=P)),
                    (c0[:], cos0.rearrange("(t p) c -> p t c", p=P)),
                    (s0[:], sin0.rearrange("(t p) c -> p t c", p=P))):
                e.dma_start(dst, src).then_inc(loaded, 16)
            for dst, src in (
                    (raw1.rearrange("p (k f) -> p k f", k=KC), w1.rearrange("(k p) f -> p k f", p=P)),
                    (raw2.rearrange("p (k f) -> p k f", k=KC), w2.rearrange("(k p) f -> p k f", p=P)),
                    (raw3.rearrange("p (k f) -> p k f", f=DM)[:, 0:5, :], w3[0:640, :].rearrange("(k p) f -> p k f", p=P)),
                    (raw3[0:64, 5 * DM:], w3[640:704, :]),
                    (raw4.rearrange("p (k f) -> p k f", k=KC), f1w1.rearrange("(k p) f -> p k f", p=P)),
                    (raw5.rearrange("p (k f) -> p k f", f=DM), f1w2.rearrange("(k p) f -> p k f", p=P))):
                e.dma_start(dst, src).then_inc(raw_loaded, 16)
            for dst, src in (
                    (wo0_s[:], wo0.rearrange("(k p) f -> p k f", p=P)),
                    (mask16[:].rearrange("p a n -> p (a n)"), mask),
                    (c1[:], cos1.rearrange("(t p) c -> p t c", p=P)),
                    (s1[:].rearrange("p t a c -> p t (a c)"), sin1.rearrange("(t p) c -> p t c", p=P)),
                    (wk1_s[:], wk1.rearrange("(k p) f -> p k f", p=P)),
                    (wv1_s[:], wv1.rearrange("(k p) f -> p k f", p=P)),
                    (wq1_s[:], wq1.rearrange("(k p) f -> p k f", p=P)),
                    (wo1_s[:], wo1.rearrange("(k p) f -> p k f", p=P)),
                    (b1c[:], f1b1),
                    (b2r[:], f1b2.rearrange("(a n) -> a n", a=1).to_broadcast([P, DM]))):
                e.dma_start(dst, src).then_inc(rest_loaded, 16)
            e.drain().then_inc(x_free, 1)
            with e.Fori(0, B) as b:
                for other in names:
                    e.wait_ge(phase_end[other], at(b, PH, 3))
                with e.If(b < B - 1):
                    load_x(nc.s_assert_within(b + 1, 1, B - 1, skip_runtime_bounds_check_because="b < B - 1 here"))
                e.wait_ge(x_res, at(b, XR, XR))
                e.dma_start(out[b, :, :].rearrange("(t p) d -> p t d", p=P), x[:]).then_inc(x_stored, 16)
                e.drain().then_inc(row_end, 1)
                e.wait_ge(x_stored, 16)
                e.sem_clear(x_stored)
                e.drain().then_inc(x_free, 1)
                e.wait_ge(cleared["sp"], 1)
                e.sem_clear(cleared["sp"])

        @block.tensor
        def _(e):
            MM = pe.matmul
            e.wait_ge(loaded, 16 * NLOAD)
            e.wait_ge(consts, 2)
            with e.Fori(0, B) as b:
                enter(e, "pe", b, 0)
                for t in range(NT + 3):
                    if t < NT:
                        if t >= 2:
                            e.wait_ge(xT_ready, at(b, 16, t - 1))
                        transpose_tile(e, b, 0, t, bank(t % 2)[:, 0:2 * P].rearrange("p (k s) -> p k s", k=KC))
                    u = t - 1
                    if 0 <= u < NT:
                        e.wait_ge(xT_ready, at(b, 16, u + 1))
                        if u >= 2:
                            e.wait_ge(rope_mul, at(b, NT, u - 1))
                            e.wait_ge(v0_out, at(b, NT, u - 1))
                        for k in range(KC):
                            last = MM(bank(2 + u % 2)[:, 0:QKV0], xnT[:, k, u * P:(u + 1) * P], wqkv0_s[:, k, :],
                                      start=(k == 0), stop=(k == KC - 1))
                        last.then_inc(qkv_ready, 1)
                    u = t - 3
                    if 0 <= u < NT:
                        e.wait_ge(lo_done, at(b, NT, u + 1))
                        for c, (h0, h1) in enumerate(((0, 8), (8, 16), (16, 20))):
                            if u >= 1:
                                if c == 1:
                                    e.wait_ge(hT_act, at(b, NT, u))
                                else:
                                    e.wait_ge(hT_dve, at(b, 2 * NT, 2 * u - 1 + c // 2))
                            for h in range(h0, h1):
                                last = pe.transpose(bank16(4 + c)[0:65, (h - h0) * P:(h - h0 + 1) * P],
                                                    T16[:, u % 2, h, 0:65], id16[:])
                            last.then_inc(hT_ready, 1)
                leave(e, "pe")
                enter(e, "pe", b, 1)

                def slot(n, todo_j):
                    if n >= 2:
                        prev = {"max": (max_done, 16 * NHG), "row": (mrow_moved, NHG), "out": (o_done, NHG)}[slots[n - 2]]
                        e.wait_ge(prev[0], at(b, prev[1], nth[n - 2]))
                    pair = 2 * (n % 2)
                    if slots[n] == "max":
                        m = nth[n] - 1
                        j, h, qt = m // 16, m // 4 % 4, m % 4
                        kv, qc = j // 2, j % 2
                        for half in range(2):
                            last = MM(bank(pair + half), QT[:, 4 * kv + h, (4 * qc + qt) * P:(4 * qc + qt + 1) * P],
                                      KT[:, kv, half * HALF:(half + 1) * HALF], start=True, stop=True)
                        last.then_inc(max_ready, 1)
                    elif slots[n] == "row":
                        j = nth[n] - 1
                        e.wait_ge(max_done, at(b, 16 * NHG, 16 * (j + 1)))
                        dst = psum[64:65, pair:pair + 2, :].rearrange("p a n -> p (a n)").bitcast(F16)
                        for i in range(16):
                            last = pe.matmul(dst[:, i * P:(i + 1) * P], mneg[:, j % 2, i:i + 1], id16[:],
                                             start=True, stop=True, is_transpose=True, tile_position=(0, 64))
                        last.then_inc(mrow_ready, 1)
                    else:
                        j = nth[n] - 1
                        e.wait_ge(osum_done, at(b, NHG, j + 1))
                        for i in range(4):
                            last = pe.transpose(bank(pair)[:, i * P:(i + 1) * P], osum[:, i * P:(i + 1) * P], id32[:])
                        last.then_inc(oTr_ready, 1)

                def products(j, kt):
                    n0 = (j * NK + kt) * G0
                    if kt == 0 and j >= 1:
                        e.wait_ge(osum_done, at(b, NHG, j))
                    e.wait_ge(exp_done, at(b, 4 * NHG * NK, n0 + G0))
                    for h in range(G0):
                        last = MM(psum[32 * h:32 * h + 32, 7, :], V0[:, kt, j // 2, :], prob0[:, (n0 + h) % PR, :],
                                  start=(kt == 0), stop=(kt == NK - 1), tile_position=(0, 32 * h))
                    last.then_inc(pv_done, 1)

                for n in range(first_slots):
                    slot(n, 0)
                for j in range(NHG):
                    e.wait_ge(mrow_moved, at(b, NHG, j + 1))
                    for kt in range(NK):
                        n0 = (j * NK + kt) * G0
                        base, todo = plan[j][kt]
                        left = list(range(base, base + len(todo)))
                        for h in range(G0):
                            n = n0 + h
                            if n >= 3:
                                e.wait_ge(exp_done, at(b, 4 * NHG * NK, n - 2))
                            MM(bank(4 + n % 3), KT[:, j // 2, kt * P:(kt + 1) * P],
                               QT[:, 4 * (j // 2) + h, (j % 2) * HALF:(j % 2 + 1) * HALF],
                               start=True, stop=True).then_inc(st_ready, 1)
                            if h % 2 == 1 and left:
                                slot(left.pop(0), j)
                        if kt >= 1:
                            products(j, kt - 1)
                        elif j >= 1:
                            products(j - 1, NK - 1)
                        while left:
                            slot(left.pop(0), j)
                products(NHG - 1, NK - 1)
                slot(len(slots) - 1, NHG)
                leave(e, "pe")
                enter(e, "pe", b, 2)
                e.wait_ge(rest_loaded, 16 * NREST)
                e.wait_ge(quant, 1)
                for t in range(NT + 1):
                    if t < NT:
                        if t >= 2:
                            e.wait_ge(ot_moved, at(b, NT, t - 1))
                        for k in range(KC):
                            last = pe.transpose(bank(4 + t % 2)[:, k * P:(k + 1) * P], otok[:, t, k * P:(k + 1) * P], id32[:])
                        last.then_inc(ot_ready, 1)
                    u = t - 1
                    if u >= 0:
                        e.wait_ge(ot_moved, at(b, NT, u + 1))
                        if u >= 2:
                            e.wait_ge(x_res, at(b, XR, u - 1))
                        for k in range(KC):
                            last = MM(bank(2 + u % 2)[:, 0:DM], oT[:, u % 2, k * P:(k + 1) * P], wo0_s[:, k, :],
                                      start=(k == 0), stop=(k == KC - 1))
                        last.then_inc(wo_ready, 1)
                    if t == TURN_T:
                        turn_chunk(e, b, 0, 0)
                ffn_pe(e, b, 0)
                leave(e, "pe")
                enter(e, "pe", b, 3)

                def bank3(idx):
                    if idx >= 1:
                        e.wait_ge(tr_moved, at(b, NTR, idx))

                def turn(idx, kind, n):
                    bank3(idx)
                    if kind == "x":
                        transpose_tile(e, b, 2, n, bank(3)[:, 0:2 * P].rearrange("p (k s) -> p k s", k=KC))
                    else:
                        e.wait_ge(pj_rot, at(b, NPC * NT, n + 1))
                        for c in range(4):
                            last = pe.transpose(bank(3)[:, c * P:(c + 1) * P], rot[:, n % 2, c * P:(c + 1) * P], id32[:])
                        last.then_inc(tr_ready, 1)

                def project(n):
                    s, i = n // NPC, n % NPC
                    if i == 0:
                        idx = tr_plan.index(("x", s))
                        e.wait_ge(tr_moved, at(b, NTR, idx + 1))
                    if n >= 2:
                        e.wait_ge(pj_read, at(b, NPC * NT, n - 1))
                    w = wq1_s[:, :, i * NR:(i + 1) * NR] if i < NPC - 1 else wk1_s[:]
                    for k in range(KC):
                        last = MM(bank(n % 2), xnT[:, k, s * P:(s + 1) * P], w[:, k, :], start=(k == 0), stop=(k == KC - 1))
                    last.then_inc(pj_ready, 1)

                def values(s):
                    if s >= 1:
                        e.wait_ge(vp_moved, at(b, NT, s))
                    for k in range(KC):
                        last = MM(bank(2), xnT[:, k, s * P:(s + 1) * P], wv1_s[:, k, :], start=(k == 0), stop=(k == KC - 1))
                    last.then_inc(vp_ready, 1)

                def scores(s, gp):
                    e.wait_ge(tr_moved, at(b, NTR, tr_plan.index(("q", NPC * s + NPC - 1)) + 1))
                    n = GP1 * s + gp
                    if n >= 2:
                        e.wait_ge(sT_done, at(b, 4 * NT, n - 1))
                    first = 1 if s == 0 else 0
                    MM(bank(4 + n % 2), id16[:], mask16[:, first, :], start=True, stop=False, skip_group_check=True)
                    for q in range(NQB):
                        for part in range(1 if first and q == 0 else 2):
                            kb = NQB * s + q - part
                            for ev in range(2):
                                quad = 32 * (2 * part + ev)
                                last = MM(psum[quad:quad + 32, 4 + n % 2, q * P:(q + 1) * P],
                                          Kz[:, gp, ev, kb // NQB % KR, (kb % NQB) * QB:(kb % NQB + 1) * QB],
                                          QT1[:, 4 * gp:4 * gp + 4, q * QB:(q + 1) * QB],
                                          start=False, stop=True, tile_position=(0, quad), skip_group_check=True)
                    last.then_inc(sc_ready, 1)

                def outputs(s, gp):
                    n = GP1 * s + gp
                    if n >= 1:
                        e.wait_ge(pv1_moved, at(b, 4 * NT, n))
                    e.wait_ge(pT_done, at(b, 4 * NT, n + 1))
                    for q in range(NQB):
                        o = bank(6).rearrange("p (h s) -> p h s", h=G1)[:, :, q * QB:(q + 1) * QB]
                        last = MM(o, Vb[:, (NQB * s + q) % (VR * NQB), gp, :],
                                  PT[:, gp, q * P:(q + 1) * P].rearrange("p (h s) -> p h s", h=G1), start=True, stop=True)
                    last.then_inc(pv1_ready, 1)

                def out_project(s, gp):
                    e.wait_ge(pv1_moved, at(b, 4 * NT, 4 * s + gp + 1))
                    if gp == 0 and s >= 1:
                        e.wait_ge(x_res, at(b, XR, 16 + s))
                    for c in range(4 * gp, 4 * gp + 4):
                        last = MM(bank(7)[:, 0:DM], OT1[:, c // 4, c % 4, :], wo1_s[:, c, :],
                                  start=(c == 0), stop=(c == 15))
                    if gp == GP1 - 1:
                        last.then_inc(wo_ready, 1)

                turn(0, "x", 0)
                for s in range(NT + 2):
                    if s == NT + 1:
                        e.wait_ge(pj_read, at(b, NPC * NT, NPC * NT))
                        turn_chunk(e, b, 1, 0)
                    for i in range(NPC):
                        n = NPC * s + i
                        if n < NPC * NT:
                            project(n)
                        todo = list(steps[s][i])
                        if todo and todo[0][1] == "x":
                            turn(*todo.pop(0))
                        if i == NPC - 1 and 2 <= s <= NT:
                            for gp in range(GP1):
                                out_project(s - 2, gp)
                        for g in todo:
                            turn(*g)
                        if i == 1:
                            if s < NT:
                                values(s)
                            for u in range(4):
                                if 1 <= s <= NT:
                                    scores(s - 1, u)
                                if s >= 2:
                                    outputs(s - 2, u)
                                if s == NT + 1 and u >= 1:
                                    out_project(s - 2, u - 1)
                            if s == NT + 1:
                                out_project(s - 2, GP1 - 1)
                leave(e, "pe")
                enter(e, "pe", b, 4)
                ffn_pe(e, b, 1)
                end_row(e, "pe")

        @block.scalar
        def _(e):
            with e.Fori(0, B) as b:
                enter(e, "act", b, 0)
                e.wait_ge(x_free, 1)
                e.sem_clear(x_free)
                for t in range(NT + 3):
                    if t < NT:
                        e.wait_ge(xn_moved, at(b, 32, t + 1))
                        act.copy(xnT[:, :, t * P:(t + 1) * P],
                                 bank(t % 2)[:, 0:2 * P].rearrange("p (k s) -> p k s", k=KC)).then_inc(xT_ready, 1)
                        act.copy(x[:, t, :], otok[:, t, :]).then_inc(x_copied, 1)
                    u = t - 1
                    if 0 <= u < NT:
                        e.wait_ge(qkv_ready, at(b, NT, u + 1))
                        if u >= 2:
                            e.wait_ge(lo_done, at(b, NT, u - 1))
                        ps = bank(2 + u % 2)
                        if u == 0:
                            e.wait_ge(prep, at(b, 7, 4))
                        act.copy(qk32[:, u % 2, :, 8:16],
                                 ps[:, 0:HD0 * D0].rearrange("p (h d) -> p h d", d=D0)[:, :, 8:16])
                        act.copy(V0[:, u, :, 0:D0],
                                 ps[:, HD0 * D0:QKV0].rearrange("p (h d) -> p h d", d=D0)).then_inc(v0_out, 1)
                    u = t - 2
                    if 0 <= u < NT:
                        e.wait_ge(rope_done, at(b, NT, u + 1))
                        e.wait_ge(v0_out, at(b, NT, u + 1))
                        if u >= 2:
                            e.wait_ge(hT_ready, at(b, 3 * NT, 3 * (u - 1)))
                        if u == 0:
                            e.wait_ge(prep, at(b, 7, 2))
                        q16 = T16[:, u % 2, 0:H0, 0:64].rearrange("p h (r d) -> p h r d", r=4)
                        k16 = T16[:, u % 2, H0:HD0, 0:64].rearrange("p h (r d) -> p h r d", r=4)
                        act.copy(q16[:, :, 0:4:2, :], qk32[:, u % 2, 0:H0, :].unsqueeze(2).to_broadcast([P, H0, 2, D0]))
                        act.copy(k16[:, :, 0:2, :], qk32[:, u % 2, H0:HD0, :].unsqueeze(2).to_broadcast([P, KV0, 2, D0])
                                 ).then_inc(hi_done, 1)
                    u = t - 3
                    if 0 <= u < NT:
                        if u == 0:
                            e.wait_ge(prep, at(b, 7, 7))
                        e.wait_ge(hT_ready, at(b, 3 * NT, 3 * u + 2))
                        act.copy(QT[0:65, 8:16, u * P:(u + 1) * P],
                                 bank16(5)[0:65, :].rearrange("p (h s) -> p h s", h=8)).then_inc(hT_act, 1)
                leave(e, "act")
                enter(e, "act", b, 1)

                def row(j):
                    pair = 2 * (slot_of("row", j) % 2)
                    e.wait_ge(mrow_ready, at(b, NHG, j + 1))
                    src = psum[64:65, pair:pair + 2, :].rearrange("p a n -> p (a n)").bitcast(F16)
                    act.copy(QT[64:65, 4 * (j // 2):4 * (j // 2) + 4, (j % 2) * HALF:(j % 2 + 1) * HALF],
                             src.rearrange("p (h s) -> p h s", h=4)).then_inc(mrow_moved, 1)

                with e.If(b < 1):
                    e.wait_ge(raw_loaded, 16 * NRAW)
                    e.wait_ge(wzero, 1)
                    junk = otok[:].rearrange("p t d -> p (t d)")
                    for i, (rows, raw) in enumerate(((P, raw1), (P, raw2), (P, raw3[:, 0:5 * DM]), (P, raw4), (P, raw5),
                                                     (64, raw3[0:64, 5 * DM:]))):
                        if i:
                            e.wait_ge(absdone, i)
                        act.activation(junk[0:rows, 0:raw.shape[1]], raw, ACT.Abs,
                                       accum_out=wabs[0:rows, i:i + 1]).then_inc(absdone, 1)
                    e.wait_ge(absdone, 6)
                def output_sums(j):
                    e.wait_ge(pv_done, at(b, NHG * NK, (j + 1) * NK))
                    if j >= 1:
                        e.wait_ge(oTr_ready, at(b, NHG, j))
                    act.copy(osum, bank(7)).then_inc(osum_done, 1)

                row(0)
                for j in range(NHG):
                    for i in range(NK * G0):
                        n = j * NK * G0 + i
                        if i == SUM_ACT and j >= 1:
                            output_sums(j - 1)
                        if i == ROW_ACT and j + 1 < NHG:
                            row(j + 1)
                        e.wait_ge(st_ready, at(b, 4 * NHG * NK, n + 1))
                        if n >= PR:
                            e.wait_ge(pv_done, at(b, NHG * NK, (n - PR) // G0 + 1))
                        act.activation(prob0[:, n % PR, :], bank(4 + n % 3), ACT.Exp, scale=float(D0) ** -0.5
                                       ).then_inc(exp_done, 1)
                output_sums(NHG - 1)
                leave(e, "act")
                enter(e, "act", b, 2)
                for t in range(NT):
                    e.wait_ge(ot_ready, at(b, NT, t + 1))
                    if t >= 2:
                        e.wait_ge(wo_ready, at(b, 2 * NT, t - 1))
                    act.copy(oT[:, t % 2, :], bank(4 + t % 2)[:, 0:DM]).then_inc(ot_moved, 1)
                    if t == TURN_T:
                        high_chunk(e, b, 0, 0)
                ffn_act(e, b, 0)
                leave(e, "act")
                enter(e, "act", b, 3)
                e.wait_ge(rest_loaded, 16 * NREST)

                def move(idx, kind, n):
                    if kind == "x":
                        e.wait_ge(xn_moved, at(b, 32, 16 + n + 1))
                        act.copy(xnT[:, :, n * P:(n + 1) * P],
                                 bank(3)[:, 0:2 * P].rearrange("p (k s) -> p k s", k=KC)).then_inc(tr_moved, 1)
                        return
                    e.wait_ge(tr_ready, at(b, NPC * NT, n + 1))
                    s, i = n // NPC, n % NPC
                    src = bank(3).rearrange("p (c s) -> p c s", c=4)
                    if i < NPC - 1:
                        if s >= 1:
                            e.wait_ge(sc_ready, at(b, 4 * NT, 4 * s))
                        act.copy(QT1[:, 4 * i:4 * i + 4, :], src).then_inc(tr_moved, 1)
                    else:
                        if s == 0:
                            e.wait_ge(prep4, at(b, 3, 3))
                        if s >= 2:
                            e.wait_ge(sc_ready, at(b, 4 * NT, 4 * (s - 1)))
                        act.copy(Kz[0:64, :, 0, s % KR, :], src[0:64, :, :])
                        act.copy(Kz[64:P, :, 1, s % KR, :], src[64:P, :, :]).then_inc(tr_moved, 1)

                def exps(s, u):
                    n = 4 * s + u
                    e.wait_ge(sub_done, at(b, 4 * NT, n + 1))
                    act.activation(sE[:, n % 2, :], sE[:, n % 2, :], ACT.Exp, scale=float(D1) ** -0.5).then_inc(ex_done, 1)

                move(0, "x", 0)
                for s in range(NT + 2):
                    if s == NT + 1:
                        e.wait_ge(pj_rot, at(b, NPC * NT, NPC * NT))
                        high_chunk(e, b, 1, 0)
                    for i in range(NPC):
                        for g in steps[s][i]:
                            move(*g)
                        if i == 1:
                            for gp in range(GP1 if s >= 2 else 0):
                                e.wait_ge(pv1_ready, at(b, 4 * NT, 4 * (s - 2) + gp + 1))
                                if s >= 3:
                                    e.wait_ge(wo_ready, at(b, 2 * NT, NT + s - 2))
                                act.copy(OT1[:, gp, :, :], bank(6).rearrange("p (h s) -> p h s", h=G1)).then_inc(pv1_moved, 1)
                                if gp == 1 and s <= NT:
                                    exps(s - 1, 0)
                                    exps(s - 1, 1)
                            if s == 1:
                                exps(0, 0)
                                exps(0, 1)
                        if i in (1, 2) and s < NT:
                            e.wait_ge(vp_ready, at(b, NT, s + 1))
                            if s == 0:
                                e.wait_ge(prep4, at(b, 3, 3))
                            if s >= VR:
                                e.wait_ge(pv1_ready, at(b, 4 * NT, 4 * (s - 2)))
                            for q in range(2 * (i - 1), 2 * (i - 1) + 2):
                                src = psum[32 * q:32 * q + 32, 2, :].rearrange("p (g e d) -> p g e d", e=2, d=D1)
                                for part in range(1 if NQB * s + q == NQB * NT - 1 else 2):
                                    for ev in range(2):
                                        quad = 32 * (2 * part + ev)
                                        last = act.copy(Vb[quad:quad + 32, (NQB * s + q + part) % (VR * NQB), :,
                                                           ev * D1:(ev + 1) * D1], src[:, :, ev, :])
                            if i == 2:
                                last.then_inc(vp_moved, 1)
                        if i in (3, 4) and 1 <= s <= NT:
                            exps(s - 1, i - 1)
                leave(e, "act")
                enter(e, "act", b, 4)
                ffn_act(e, b, 1)
                end_row(e, "act")

        @block.vector
        def _(e):
            e.wait_ge(loaded, 16 * NLOAD)
            with e.Fori(0, B) as b:
                enter(e, "dve", b, 0)
                e.wait_ge(x_loaded, 32)
                LEAD = 4
                for t in range(-LEAD, NT + 3):
                    if t + LEAD < NT:
                        ln_stats(e, b, 0, t + LEAD, None)
                    if 0 <= t + LEAD - 1 < NT:
                        ln_norm(e, b, 0, t + LEAD - 1)
                    u = t - 1
                    if 0 <= u < NT:
                        e.wait_ge(v0_out, at(b, NT, u + 1))
                        if u >= 2:
                            e.wait_ge(hi_done, at(b, NT, u - 1))
                        if u >= 1:
                            e.wait_ge(rope_done, at(b, NT, u))
                        qk = bank(2 + u % 2)[:, 0:HD0 * D0].rearrange("p (h d) -> p h d", d=D0)[:, :, 0:8]
                        pair = qk.rearrange("p h (i two) -> p h i two", two=2)
                        rb = ropeB.rearrange("p h (i two) -> p h i two", two=2)
                        sn = s0[:, u, :].rearrange("p (i two) -> p i two", two=2)
                        dve.tensor_tensor(ropeA, qk, c0[:, u, :].unsqueeze(1).to_broadcast([P, HD0, 8]), ALU.mult)
                        for o in range(2):
                            last = dve.tensor_tensor(rb[:, :, :, o], pair[:, :, :, 1 - o],
                                                     sn[:, :, o].unsqueeze(1).to_broadcast([P, HD0, 4]), ALU.mult)
                        last.then_inc(rope_mul, 1)
                        e.wait_ge(rope_mul, at(b, NT, u + 1))
                        dve.tensor_tensor(qk32[:, u % 2, :, 0:8], ropeA, ropeB, ALU.add).then_inc(rope_done, 1)
                    u = t - 2
                    if 0 <= u < NT:
                        e.wait_ge(hi_done, at(b, NT, u + 1))
                        q16 = T16[:, u % 2, 0:H0, 0:64].rearrange("p h (r d) -> p h r d", r=4)
                        k16 = T16[:, u % 2, H0:HD0, 0:64].rearrange("p h (r d) -> p h r d", r=4)
                        dve.tensor_tensor(q16[:, :, 1:4:2, :], qk32[:, u % 2, 0:H0, :].unsqueeze(2).to_broadcast([P, H0, 2, D0]),
                                          q16[:, :, 0:4:2, :], ALU.subtract)
                        dve.tensor_tensor(k16[:, :, 2:4, :], qk32[:, u % 2, H0:HD0, :].unsqueeze(2).to_broadcast([P, KV0, 2, D0]),
                                          k16[:, :, 0:2, :], ALU.subtract).then_inc(lo_done, 1)
                    u = t - 3
                    if 0 <= u < NT:
                        if u == 0:
                            e.wait_ge(prep, at(b, 7, 7))
                        e.wait_ge(hT_ready, at(b, 3 * NT, 3 * u + 1))
                        dve.tensor_copy(QT[0:65, 0:8, u * P:(u + 1) * P],
                                        bank16(4)[0:65, :].rearrange("p (h s) -> p h s", h=8)).then_inc(hT_dve, 1)
                        e.wait_ge(hT_ready, at(b, 3 * NT, 3 * u + 3))
                        dve.tensor_copy(KT[0:65, :, u * P:(u + 1) * P],
                                        bank16(6)[0:65, 0:4 * P].rearrange("p (h s) -> p h s", h=4)).then_inc(hT_dve, 1)
                leave(e, "dve")
                enter(e, "dve", b, 1)
                e.wait_ge(x_copied, at(b, NT, NT))
                e.sem_clear(x_loaded)
                for n, kind in enumerate(slots):
                    pair = 2 * (n % 2)
                    if kind == "max":
                        m = nth[n] - 1
                        j = m // 16
                        e.wait_ge(max_ready, at(b, 16 * NHG, m + 1))
                        if m % 16 == 0 and j >= 2:
                            e.wait_ge(mrow_ready, at(b, NHG, j - 1))
                        with nc.allow_low_precision(reason="a stabiliser: the same rounded value is in numerator and denominator"):
                            dve.tensor_reduce(mneg[:, j % 2, m % 16:m % 16 + 1], psum[:, pair:pair + 2, :], AX.XY, ALU.max,
                                              negate=True).then_inc(max_done, 1)
                    elif kind == "out":
                        j = nth[n] - 1
                        e.wait_ge(oTr_ready, at(b, NHG, j + 1))
                        o = bank(pair).rearrange("p (m d) -> p m d", d=32)
                        if j >= 1:
                            e.wait_ge(o_done, at(b, NHG, j))
                        dve.reciprocal(orec, o[:, :, D0]).then_inc(orec_done, 1)
                        e.wait_ge(orec_done, at(b, NHG, j + 1))
                        dst = otok[:, 4 * (j % 2):4 * (j % 2) + 4, (j // 2) * 64:(j // 2 + 1) * 64].rearrange(
                            "p t (h d) -> p t h d", d=D0)
                        dve.tensor_tensor(dst, o[:, :, 0:D0].rearrange("p (t h) d -> p t h d", h=4),
                                          orec.rearrange("p (t h) -> p t h", h=4).unsqueeze(3).to_broadcast([P, 4, 4, D0]),
                                          ALU.mult).then_inc(o_done, 1)
                leave(e, "dve")
                enter(e, "dve", b, 2)
                for t in range(NT + 1):
                    if t < NT:
                        e.wait_ge(wo_ready, at(b, 2 * NT, t + 1))
                        dve.tensor_tensor(x[:, t, :], bank(2 + t % 2)[:, 0:DM], x[:, t, :], ALU.add).then_inc(x_res, 1)
                        ln_stats(e, b, 1, t, t + 1)
                    if t >= 1:
                        ln_norm(e, b, 1, t - 1)
                    if t == TURN_T:
                        low_chunk(e, b, 0, 0)
                ffn_dve(e, b, 0)
                leave(e, "dve")
                enter(e, "dve", b, 3)
                e.wait_ge(rest_loaded, 16 * NREST)

                def rope(n):
                    s = n // NPC
                    e.wait_ge(pj_ready, at(b, NPC * NT, n + 1))
                    if n >= 2:
                        e.wait_ge(pj_rot, at(b, NPC * NT, n - 1))
                    ps = bank(n % 2)
                    dve.tensor_tensor(rA[:, n % 2, :].rearrange("p (h c) -> p h c", c=32), ps.rearrange("p (h c) -> p h c", c=32),
                                      c1[:, s, :].unsqueeze(1).to_broadcast([P, 16, 32]), ALU.mult)
                    half = ps.rearrange("p (h a c) -> p h a c", a=2, c=32)
                    rb = rB[:, n % 2, :].rearrange("p (h a c) -> p h a c", a=2, c=32)
                    for a in range(2):
                        last = dve.tensor_tensor(rb[:, :, a, :], half[:, :, 1 - a, :],
                                                 s1[:, s, a, :].unsqueeze(1).to_broadcast([P, 8, 32]), ALU.mult)
                    last.then_inc(pj_read, 1)

                def both_parts(dst, src, n, op, done):
                    own, before = src[0:64, n % 2, :], src[64:P, n % 2, :]
                    dve.tensor_tensor(dst[0:64, n % 2, :], own, before, op)
                    dve.tensor_tensor(dst[64:P, n % 2, :], own, before, op).then_inc(done, 1)

                def turn_max(s, u):
                    n = 4 * s + u
                    e.wait_ge(sc_ready, at(b, 4 * NT, n + 1))
                    if n >= 2:
                        e.wait_ge(sub_done, at(b, 4 * NT, n - 1))
                    dve.transpose(sT[:, n % 2, :], bank(4 + n % 2)).then_inc(sT_done, 1)
                    e.wait_ge(sT_done, at(b, 4 * NT, n + 1))
                    dve.tensor_reduce(smax[:, n % 2, :], sT[:, n % 2, :].rearrange("p (m c) -> p m c", c=QB), AX.X, ALU.max
                                      ).then_inc(mx_done, 1)
                    e.wait_ge(mx_done, at(b, 4 * NT, n + 1))
                    both_parts(mboth, smax, n, ALU.max, mb_done)

                def sums(s, u):
                    n = 4 * s + u
                    e.wait_ge(ex_done, at(b, 4 * NT, n + 1))
                    if n >= 2:
                        e.wait_ge(nrm_done, at(b, 4 * NT, n - 1))
                    dve.tensor_reduce(ssum[:, n % 2, :], sE[:, n % 2, :].rearrange("p (m c) -> p m c", c=QB), AX.X, ALU.add
                                      ).then_inc(sm_done, 1)
                    e.wait_ge(sm_done, at(b, 4 * NT, n + 1))
                    both_parts(sboth, ssum, n, ALU.add, sb_done)
                    e.wait_ge(sb_done, at(b, 4 * NT, n + 1))
                    dve.reciprocal(sboth[:, n % 2, :], sboth[:, n % 2, :]).then_inc(rc_done, 1)

                def turn_back(s, u):
                    n = 4 * s + u
                    e.wait_ge(nrm_done, at(b, 4 * NT, n + 1))
                    if u == 0 and s >= 1:
                        e.wait_ge(pv1_ready, at(b, 4 * NT, 4 * s))
                    dve.transpose(PT[:, u, :], sE[:, n % 2, :]).then_inc(pT_done, 1)

                for s in range(NT + 2):
                    if s == NT + 1:
                        low_chunk(e, b, 1, 0)
                    live = 1 <= s <= NT
                    for i in range(NPC):
                        if s < NT:
                            rope(NPC * s + i)
                        if i == 1 and live:
                            turn_max(s - 1, 0)
                            turn_max(s - 1, 1)
                        if i == 2 and live:
                            sums(s - 1, 0)
                            sums(s - 1, 1)
                            turn_max(s - 1, 2)
                        if i == 3 and live:
                            turn_max(s - 1, 3)
                            turn_back(s - 1, 0)
                            sums(s - 1, 2)
                            turn_back(s - 1, 1)
                        if i == 4 and live:
                            sums(s - 1, 3)
                            turn_back(s - 1, 2)
                            turn_back(s - 1, 3)
                    if s >= 2:
                        t = s - 2
                        e.wait_ge(wo_ready, at(b, 2 * NT, NT + t + 1))
                        dve.tensor_tensor(x[:, t, :], bank(7)[:, 0:DM], x[:, t, :], ALU.add).then_inc(x_res, 1)
                        ln_stats(e, b, 3, t, 16 + t + 1)
                        if t >= 1:
                            ln_norm(e, b, 3, t - 1)
                ln_norm(e, b, 3, NT - 1)
                leave(e, "dve")
                enter(e, "dve", b, 4)
                ffn_dve(e, b, 1)
                end_row(e, "dve")

        def ternary(e):
            e.wait_ge(absdone, 6)
            pool.partition_all_reduce(wtot[:, 0:6], wabs[:, 0:6], P, bass.bass_isa.ReduceOp.add).then_inc(absall, 1)
            e.wait_ge(absall, 1)
            pool.tensor_tensor(wtot[:, 2:3], wtot[:, 2:3], wtot[:, 5:6], ALU.add).then_inc(absall, 1)
            e.wait_ge(absall, 2)
            pool.tensor_scalar(thr[:, 2, 0:3], wtot[:, 0:3], 1.0 / (DM * F0), 1e-8, ALU.mult, ALU.add).then_inc(thrdone, 1)
            pool.tensor_scalar(thr[:, 0, 3:5], wtot[:, 3:5], 1.0 / (DM * F1), 0.7, ALU.mult, ALU.mult).then_inc(thrdone, 1)
            e.wait_ge(thrdone, 2)
            pool.tensor_scalar(thr[:, 0, 0:3], thr[:, 2, 0:3], 0.5, None, ALU.mult).then_inc(thrdone, 1)
            e.wait_ge(thrdone, 3)
            pool.tensor_scalar(thr[:, 1, :], thr[:, 0, :], -1.0, None, ALU.mult).then_inc(thrdone, 1)
            e.wait_ge(thrdone, 4)
            flat = "p k f -> p (k f)"
            pieces = ((0, P, raw1, t1[:].rearrange(flat)), (1, P, raw2, t2[:].rearrange(flat)),
                      (2, P, raw3[:, 0:5 * DM], t3[:, 0:5, :].rearrange(flat)), (2, 64, raw3[0:64, 5 * DM:], t3[0:64, 5, :]),
                      (3, P, raw4, u1[:].rearrange(flat)), (4, P, raw5, u2[:].rearrange(flat)))
            done = 0
            for i, rows, raw, q in pieces:
                gt, lt = (ALU.is_gt, ALU.is_lt) if i < 3 else (ALU.is_ge, ALU.is_le)
                less = below[0:rows, 0:raw.shape[1]]
                if done:
                    e.wait_ge(qstep, done)
                pool.tensor_scalar(q, raw, thr[0:rows, 0, i:i + 1], None, gt).then_inc(qstep, 1)
                e.wait_ge(qstep, done + 1)
                pool.tensor_scalar(less, raw, thr[0:rows, 1, i:i + 1], None, lt).then_inc(qstep, 1)
                e.wait_ge(qstep, done + 2)
                pool.tensor_tensor(q, q, less, ALU.subtract).then_inc(qstep, 1)
                done += 3
            e.wait_ge(qstep, done)
            e.drain().then_inc(quant, 1)

        @block.gpsimd
        def _(e):
            pool.memset(mhalf[:], -0.5).then_inc(consts, 1)
            pool.memset(wabs[:], 0.0).then_inc(wzero, 1)
            e.wait_ge(loaded, 16 * NLOAD)
            pool.tensor_copy(id16[:], id32[:]).then_inc(consts, 1)
            e.wait_ge(consts, 2)
            with e.Fori(0, B) as b:
                enter(e, "pool", b, 0)
                u32 = mybir.dt.uint32
                fills = ((T16[:, :, 0:H0, 64:65], 0.0), (T16[:, :, H0:HD0, 64:65], 1.0),
                         (V0[:, :, :, D0 + 1:32], 0.0), (V0[:, :, :, D0:D0 + 1], 1.0),
                         (QT[64:P, 0:8, :].bitcast(u32), 0), (KT[64:P, :, :].bitcast(u32), 0),
                         (QT[64:P, 8:16, :].bitcast(u32), 0))

                def fill(first, last):
                    for i in range(first, last):
                        if i:
                            e.wait_ge(prep, i)
                        pool.memset(fills[i][0], fills[i][1]).then_inc(prep, 1)
                    e.wait_ge(prep, at(b, 7, last))

                big_fills = (3, 4, 6)
                for t in range(NT):
                    ln_pow(e, b, 0, t)
                    e.wait_ge(rstd_ready, at(b, 32, t + 1))
                    if t == 1:
                        fill(0, 4)
                    if t in big_fills:
                        fill(4 + big_fills.index(t), 5 + big_fills.index(t))
                leave(e, "pool")
                enter(e, "pool", b, 1)
                with e.If(b < 1):
                    ternary(e)
                leave(e, "pool")
                enter(e, "pool", b, 2)
                e.wait_ge(rest_loaded, 16 * NREST)
                for t in range(NT):
                    ln_pow(e, b, 1, t)
                ffn_pool(e, b, 0)
                for t in range(NT):
                    ln_pow(e, b, 2, t)
                leave(e, "pool")
                enter(e, "pool", b, 3)
                for i, dst in enumerate((Kz[0:64, :, 1, :, :], Kz[64:P, :, 0, :, :], Vb)):
                    if i:
                        e.wait_ge(prep4, i)
                    pool.memset(dst, 0.0).then_inc(prep4, 1)

                def rotate(n):
                    e.wait_ge(pj_read, at(b, NPC * NT, n + 1))
                    if n >= 2:
                        e.wait_ge(tr_ready, at(b, NPC * NT, n - 1))
                    pool.tensor_tensor(rot[:, n % 2, :], rA[:, n % 2, :], rB[:, n % 2, :], ALU.add).then_inc(pj_rot, 1)

                def minus_max(s, u):
                    n = 4 * s + u
                    e.wait_ge(mb_done, at(b, 4 * NT, n + 1))
                    if n >= 2:
                        e.wait_ge(pT_done, at(b, 4 * NT, n - 1))
                    pool.tensor_tensor(sE[:, n % 2, :].rearrange("p (m c) -> p m c", c=QB),
                                       sT[:, n % 2, :].rearrange("p (m c) -> p m c", c=QB),
                                       mboth[:, n % 2, :].unsqueeze(2).to_broadcast([P, NM, QB]), ALU.subtract).then_inc(sub_done, 1)

                def normalise(s, u):
                    n = 4 * s + u
                    e.wait_ge(rc_done, at(b, 4 * NT, n + 1))
                    v = sE[:, n % 2, :].rearrange("p (m c) -> p m c", c=QB)
                    pool.tensor_tensor(v, v, sboth[:, n % 2, :].unsqueeze(2).to_broadcast([P, NM, QB]), ALU.mult).then_inc(nrm_done, 1)

                for s in range(NT + 2):
                    live = 1 <= s <= NT
                    for i in range(NPC):
                        if s < NT:
                            rotate(NPC * s + i)
                        if live and i == 1:
                            minus_max(s - 1, 0)
                            minus_max(s - 1, 1)
                        if live and i == 2:
                            normalise(s - 1, 0)
                            normalise(s - 1, 1)
                        if live and i == 3:
                            minus_max(s - 1, 2)
                            minus_max(s - 1, 3)
                        if live and i == 4:
                            normalise(s - 1, 2)
                            normalise(s - 1, 3)
                    if s >= 2:
                        ln_pow(e, b, 3, s - 2)
                leave(e, "pool")
                enter(e, "pool", b, 4)
                ffn_pool(e, b, 1)
                e.wait_ge(row_end, 4)
                pool.sem_clear(row_sems)
                for other in cleared:
                    e.drain().then_inc(cleared[other], 1)


def tables():
    pos = np.arange(S, dtype=np.float32)
    inv0 = (1.0 / 10000.0 ** (np.arange(0, D0 // 2, 2, dtype=np.float32) / np.float32(D0 // 2))).astype(np.float32)
    a0 = pos[:, None] * inv0[None, :]
    cos0 = np.repeat(np.cos(a0), 2, axis=1).astype(np.float32)
    sin0 = np.stack([-np.sin(a0), np.sin(a0)], axis=-1).reshape(S, 8).astype(np.float32)
    inv1 = (1.0 / 10000.0 ** (np.arange(0, D1, 2, dtype=np.float32) / np.float32(D1))).astype(np.float32)
    a1 = pos[:, None] * inv1[None, :]
    cos1 = np.cos(a1).astype(np.float32)
    sin1 = np.concatenate([-np.sin(a1), np.sin(a1)], axis=1).astype(np.float32)
    key, query = np.arange(QB)[:, None], np.arange(QB)[None, :]
    own = np.where(key <= query, 0.0, MASKED)
    before = np.where(key >= query, 0.0, MASKED)
    mask = np.zeros((2, 2, QB, 2, NQB, G1, QB), np.float16)
    for part, block in enumerate((own, before)):
        mask[part] = block[None, :, None, None, None, :]
    mask[1, :, :, 1, 0] = MASKED
    return cos0, sin0, cos1, sin1, np.eye(P, dtype=np.float32), mask.reshape(P, 2 * HALF)


def kernel(**inputs):
    import concourse.bacc as bacc
    from concourse.bass_utils import run_bass_kernel_spmd

    a = {k: np.ascontiguousarray(v) for k, v in inputs.items()}
    cos0, sin0, cos1, sin1, ident, mask = tables()
    wq1 = a["L1_attn_wq"].T.reshape(DM, GP1, 2, G1, D1).transpose(0, 1, 3, 2, 4).reshape(DM, H1 * D1)
    wo1 = a["L1_attn_wo"].T.reshape(GP1, 2, G1, D1, DM).transpose(0, 2, 1, 3, 4).reshape(H1 * D1, DM)
    arrays = {
        "x_in": a["L0_attn_hidden_states"],
        "cos0": cos0, "sin0": sin0, "cos1": cos1, "sin1": sin1, "ident": ident, "mask": mask,
        "wqkv0": np.concatenate([a["L0_attn_Wq"], a["L0_attn_Wk"], a["L0_attn_Wv"]], axis=1),
        "wo0": a["L0_attn_Wo"],
        "w1": a["L0_ffn_w1"].T, "w2": a["L0_ffn_w2"].T, "w3": a["L0_ffn_w3"].T,
        "wq1": wq1, "wk1": a["L1_attn_wk"].T, "wv1": a["L1_attn_wv"].T, "wo1": wo1,
        "f1w1": a["L1_ffn_w1"].T, "f1b1": a["L1_ffn_b1"].reshape(len(FC1), P).T, "f1w2": a["L1_ffn_w2"].T, "f1b2": a["L1_ffn_b2"],
    }
    arrays = {k: np.ascontiguousarray(v) for k, v in arrays.items()}
    nc = bacc.Bacc("TRN2", target_bir_lowering=False, num_devices=1)
    args = [nc.dram_tensor(k, v.shape, mybir.dt.from_np(v.dtype), kind="ExternalInput").ap() for k, v in arrays.items()]
    out = nc.dram_tensor("out_0", (B, S, DM), F32, kind="ExternalOutput").ap()
    build(nc, *args, out)
    r = run_bass_kernel_spmd(nc, [arrays], core_ids=[0])
    return r.results[0]["out_0"]
```
